# Optimizing a Trainium2 kernel written in Bass

```python
import numpy as np
import jax
import jax.numpy as jnp

def _softmax(x, axis=-1):
    return jax.nn.softmax(x, axis=axis)

def _gelu(x):
    return jax.nn.gelu(x, approximate=True)

def _silu(x):
    return jax.nn.silu(x)

def _sigmoid(x):
    return jax.nn.sigmoid(x)

def _layernorm(x, axis=-1, eps=1e-05):
    m = jnp.mean(x, axis=axis, keepdims=True)
    v = jnp.var(x, axis=axis, keepdims=True)
    return (x - m) / jnp.sqrt(v + eps)

def _scatter_add(tgt, idx, src, axis=0):
    return tgt.at[idx].add(src)

def _segment_sum(src, seg, n):
    return jax.ops.segment_sum(src, seg, n)
kernel_name = 'mk_decoder_preln_d1_seqx_r8_2b5367'

def setup_inputs(seed: int=0):
    np.random.seed(seed)
    _w = jnp.asarray

    def _rec_inputs():
        import jax
        import jax.numpy as jnp
        _rk = jax.random.key(seed)
        x = -0.0002928 + 1 * jax.random.normal(jax.random.fold_in(_rk, 1), (16, 64, 512), jnp.float32)
        _lenS = 64 - jax.random.randint(jax.random.fold_in(_rk, 7), (16,), 0, max(1, 64 // 4) + 1, jnp.int32)
        _lenS2 = 64 - jax.random.randint(jax.random.fold_in(_rk, 8), (16,), 0, max(1, 64 // 4) + 1, jnp.int32)
        _ctx_4096P = jax.random.normal(jax.random.fold_in(_rk, 11), (16, 16, 512), jnp.float32)
        _ctx_4096c = jax.random.dirichlet(jax.random.fold_in(_rk, 511), 0.3 * jnp.ones((16,), jnp.float32), (16, 64))
        _ctx_4096t = jnp.einsum('bsk,bkd->bsd', _ctx_4096c, _ctx_4096P)
        _ctx_4096t = _ctx_4096t * jax.lax.rsqrt(jnp.mean(jnp.square(_ctx_4096t)) + 1e-12) * 0.953939
        ctx_4096 = -2.8382e-05 + 0.999851 * (_ctx_4096t + 0.3 * jax.random.normal(jax.random.fold_in(_rk, 611), (16, 64, 512), jnp.float32))
        _validS = jnp.arange(64)[None, :] < _lenS[:, None]
        _validS2 = jnp.arange(64)[None, :] < _lenS2[:, None]
        _causal = jnp.tril(jnp.ones((64, 64), dtype=bool))
        mask_1x1xSxS2_ff0 = jnp.where(jnp.ones((1, 1, 64, 64), dtype=bool), 0.0, -1000000000.0).astype(jnp.float32)
        return (x, ctx_4096, mask_1x1xSxS2_ff0)
    x, ctx_4096, mask_1x1xSxS2_ff0 = _rec_inputs()

    def _L0_attn_setup():
        import jax, jax.numpy as jnp
        import numpy as np
        B, C, L = (64, 64, 512)
        key = jax.random.key(seed)
        x = jax.random.normal(key, (B, C, L), dtype=jnp.float32)
        return {'x': x}
    _L0_attn_all = _L0_attn_setup()
    _L0_attn_in = {k: v for k, v in _L0_attn_all.items() if k in ()}
    del _L0_attn_all

    def _L0_xattn_setup():
        import jax, jax.numpy as jnp
        import numpy as np
        B, Q, K, D = (1, 128, 6404, 512)
        H, KVH, HD = (32, 8, 128)
        GROUPS = H // KVH
        EPS = 1e-05

        def _rmsnorm(x, w):
            xf = x.astype(jnp.float32)
            var = jnp.mean(xf * xf, axis=-1, keepdims=True)
            return (xf * jax.lax.rsqrt(var + EPS)).astype(x.dtype) * w
        key = jax.random.key(seed)
        ks = jax.random.split(key, 8)
        s = 0.02
        return {'hidden_states': jax.random.normal(ks[0], (B, Q, D), jnp.float32), 'cross_attention_states': jax.random.normal(ks[1], (B, K, D), jnp.float32), 'attention_mask': jnp.zeros((B, 1, Q, K), jnp.float32), 'Wq': jax.random.normal(ks[2], (H * HD, D), jnp.float32) * s, 'Wk': jax.random.normal(ks[3], (KVH * HD, D), jnp.float32) * s, 'Wv': jax.random.normal(ks[4], (KVH * HD, D), jnp.float32) * s, 'Wo': jax.random.normal(ks[5], (D, H * HD), jnp.float32) * s, 'q_norm_w': jnp.ones((HD,), jnp.float32), 'k_norm_w': jnp.ones((HD,), jnp.float32)}
    _L0_xattn_all = _L0_xattn_setup()
    _L0_xattn_in = {k: v for k, v in _L0_xattn_all.items() if k in ('Wq', 'Wk', 'Wv', 'Wo', 'q_norm_w', 'k_norm_w')}
    del _L0_xattn_all

    def _L0_ffn_setup():
        import jax, jax.numpy as jnp
        import numpy as np
        H = 512
        I = 256
        E = 16
        TOPK = 4
        SI = 256
        key = jax.random.key(seed)
        ks = jax.random.split(key, 9)
        s = 0.02
        return {'hidden_states': jax.random.normal(ks[0], (2, 256, H), dtype=jnp.float32), 'gate_w': jax.random.normal(ks[1], (E, H), dtype=jnp.float32) * s, 'bias': jnp.zeros((E,), dtype=jnp.float32), 'Wg': jax.random.normal(ks[2], (E, I, H), dtype=jnp.float32) * s, 'Wu': jax.random.normal(ks[3], (E, I, H), dtype=jnp.float32) * s, 'Wd': jax.random.normal(ks[4], (E, H, I), dtype=jnp.float32) * s, 'Sg': jax.random.normal(ks[5], (SI, H), dtype=jnp.float32) * s, 'Su': jax.random.normal(ks[6], (SI, H), dtype=jnp.float32) * s, 'Sd': jax.random.normal(ks[7], (H, SI), dtype=jnp.float32) * s}
    _L0_ffn_all = _L0_ffn_setup()
    _L0_ffn_in = {k: v for k, v in _L0_ffn_all.items() if k in ('gate_w', 'bias', 'Wg', 'Wu', 'Wd', 'Sg', 'Su', 'Sd')}
    del _L0_ffn_all
    return {'x': x, 'ctx_4096': ctx_4096, 'mask_1x1xSxS2_ff0': mask_1x1xSxS2_ff0, 'L0_xattn_Wq': _L0_xattn_in['Wq'], 'L0_xattn_Wk': _L0_xattn_in['Wk'], 'L0_xattn_Wv': _L0_xattn_in['Wv'], 'L0_xattn_Wo': _L0_xattn_in['Wo'], 'L0_xattn_q_norm_w': _L0_xattn_in['q_norm_w'], 'L0_xattn_k_norm_w': _L0_xattn_in['k_norm_w'], 'L0_ffn_gate_w': _L0_ffn_in['gate_w'], 'L0_ffn_bias': _L0_ffn_in['bias'], 'L0_ffn_Wg': _L0_ffn_in['Wg'], 'L0_ffn_Wu': _L0_ffn_in['Wu'], 'L0_ffn_Wd': _L0_ffn_in['Wd'], 'L0_ffn_Sg': _L0_ffn_in['Sg'], 'L0_ffn_Su': _L0_ffn_in['Su'], 'L0_ffn_Sd': _L0_ffn_in['Sd']}

def reference(x, ctx_4096, mask_1x1xSxS2_ff0, L0_xattn_Wq, L0_xattn_Wk, L0_xattn_Wv, L0_xattn_Wo, L0_xattn_q_norm_w, L0_xattn_k_norm_w, L0_ffn_gate_w, L0_ffn_bias, L0_ffn_Wg, L0_ffn_Wu, L0_ffn_Wd, L0_ffn_Sg, L0_ffn_Su, L0_ffn_Sd):
    import jax
    import jax.numpy as jnp

    def _L0_attn_ref(x):
        import jax, jax.numpy as jnp
        import numpy as np
        B, C, L = (64, 64, 512)
        b, c, l = x.shape
        q = jnp.transpose(x, (2, 0, 1))
        scale = jnp.asarray(c, x.dtype) ** 0.5
        scores = jnp.einsum('lnc,lmc->lnm', q, q) / scale
        prob = jax.nn.softmax(scores, axis=-1)
        msg = jnp.einsum('lnm,lmc->lnc', prob, q)
        return x + jnp.transpose(msg, (1, 2, 0))

    def _L0_xattn_ref(hidden_states, cross_attention_states, attention_mask, Wq, Wk, Wv, Wo, q_norm_w, k_norm_w):
        import jax, jax.numpy as jnp
        import numpy as np
        B, Q, K, D = (1, 128, 6404, 512)
        H, KVH, HD = (32, 8, 128)
        GROUPS = H // KVH
        EPS = 1e-05

        def _rmsnorm(x, w):
            xf = x.astype(jnp.float32)
            var = jnp.mean(xf * xf, axis=-1, keepdims=True)
            return (xf * jax.lax.rsqrt(var + EPS)).astype(x.dtype) * w
        bsz, q_len, _ = hidden_states.shape
        kv_len = cross_attention_states.shape[1]
        q = (hidden_states @ Wq.T).reshape(bsz, q_len, H, HD).transpose(0, 2, 1, 3)
        k = (cross_attention_states @ Wk.T).reshape(bsz, kv_len, KVH, HD).transpose(0, 2, 1, 3)
        v = (cross_attention_states @ Wv.T).reshape(bsz, kv_len, KVH, HD).transpose(0, 2, 1, 3)
        q = _rmsnorm(q, q_norm_w)
        k = jnp.repeat(k, GROUPS, axis=1)
        v = jnp.repeat(v, GROUPS, axis=1)
        k = _rmsnorm(k, k_norm_w)
        scale = 1.0 / np.sqrt(HD)
        scores = jnp.einsum('bhqd,bhkd->bhqk', q, k) * scale
        scores = scores + attention_mask[:, :, :, :kv_len]
        probs = jax.nn.softmax(scores.astype(jnp.float32), axis=-1).astype(q.dtype)
        out = jnp.einsum('bhqk,bhkd->bhqd', probs, v)
        out = out.transpose(0, 2, 1, 3).reshape(bsz, q_len, H * HD)
        return out @ Wo.T

    def _L0_ffn_ref(hidden_states, gate_w, bias, Wg, Wu, Wd, Sg, Su, Sd):
        import jax, jax.numpy as jnp
        import numpy as np
        H = 512
        I = 256
        E = 16
        TOPK = 4
        SI = 256
        orig_shape = hidden_states.shape
        x = hidden_states.reshape(-1, orig_shape[-1])
        scores = jax.nn.sigmoid(x @ gate_w.T) + bias
        topk_w, topk_idx = jax.lax.top_k(scores, TOPK)
        topk_w = topk_w / (jnp.sum(topk_w, axis=-1, keepdims=True) + 1e-20)
        cw = jnp.sum(jax.nn.one_hot(topk_idx, E, dtype=x.dtype) * topk_w[..., None], axis=1)
        g = jnp.einsum('th,eih->eti', x, Wg)
        u = jnp.einsum('th,eih->eti', x, Wu)
        z = jax.nn.silu(g) * u
        zw = z * cw.T[:, :, None]
        out = jnp.einsum('eti,ehi->th', zw, Wd)
        out = out + jax.nn.silu(x @ Sg.T) * (x @ Su.T) @ Sd.T
        return out.reshape(orig_shape)
    x = x + _L0_attn_ref(_layernorm(x, axis=-1))
    x = x + _L0_xattn_ref(_layernorm(x, axis=-1), ctx_4096, mask_1x1xSxS2_ff0, L0_xattn_Wq, L0_xattn_Wk, L0_xattn_Wv, L0_xattn_Wo, L0_xattn_q_norm_w, L0_xattn_k_norm_w)
    x = x + _L0_ffn_ref(_layernorm(x, axis=-1), L0_ffn_gate_w, L0_ffn_bias, L0_ffn_Wg, L0_ffn_Wu, L0_ffn_Wd, L0_ffn_Sg, L0_ffn_Su, L0_ffn_Sd)
    return x

_drawn_inputs = setup_inputs


def setup_inputs(seed=0):
    import zlib

    import numpy as np

    out = dict(_drawn_inputs(seed))
    spreads = {'L0_xattn_q_norm_w': (1.0, 0.6),
     'L0_xattn_k_norm_w': (1.0, 0.6),
     'L0_ffn_bias': (0.0, 0.8)}
    factors = {'L0_ffn_gate_w': 8.0,
     'L0_ffn_Wg': 8.0,
     'L0_ffn_Wu': 8.0,
     'L0_ffn_Wd': 8.0,
     'L0_ffn_Sg': 4.959,
     'L0_ffn_Su': 4.857,
     'L0_ffn_Sd': 4.869}
    for name, (base, spread) in spreads.items():
        noise = np.random.default_rng([zlib.crc32(name.encode()), seed]).standard_normal(out[name].shape)
        drawn = base * np.exp(spread * noise) if base else spread * noise
        out[name] = jnp.asarray(drawn.astype(out[name].dtype))
    for name, factor in factors.items():
        out[name] = (out[name] * factor).astype(out[name].dtype)
    return out
```

```python
from contextlib import ExitStack

import concourse.bass as bass
from concourse import mybir

F32 = mybir.dt.float32
F16 = mybir.dt.float16
I32 = mybir.dt.int32
ALU = mybir.AluOpType
ACT = mybir.ActivationFunctionType
AX = mybir.AxisListType

P = 128
B, S, D = 16, 64, 512
T = B * S
NT = T // P
KC = D // P
H, G, HD = 32, 8, 128
HG = H // G
E, I = 16, 256
TOPK = 4
SHARED = E
IC = I // P
SW = 112
TS = 2 * SW
TILES = (T * TOPK + E * (TS - 1)) // TS
NS = 2 * TILES
NTK = NT * TOPK
NJT = -(-T // TS)
HI8 = 8
HROW = D + E
EPS = 1e-5
WS = 64.0
NEG = -1e30

HALF = D // 2
LG = 8
NJ = HALF // LG
BANK = 512


def ev(i, per, j):
    return i * per + (j + 1)


def decoder_kernel(nc, x_half, ctx_t, mask, wq, wkv, wo, qk_norm, gate_t, bias, wgu, wd, h_rows, out):
    with ExitStack() as ctx:
        def sb(name, shape, dt=F32):
            return ctx.enter_context(nc.sbuf_tensor(name, shape, dt))

        def sem(name):
            return ctx.enter_context(nc.semaphore(name))

        ps = ctx.enter_context(nc.psum_tensor("ps", [P, 8, BANK], F32))

        ident = sb("ident", [P, P])
        swap = sb("swap", [P, P])
        blockmask = sb("blockmask", [P, 32])
        ones = sb("ones", [P, P], F16)
        eps_ln = sb("eps_ln", [P, 1])
        eps_q = sb("eps_q", [P, 1])
        mask_sb = sb("mask_sb", [P, S])
        norm_sb = sb("norm_sb", [P, 2])
        wqk = sb("wqk", [P, 1])
        gate_st = sb("gate_st", [P, KC, E])
        gate_hi = sb("gate_hi", [P, KC, E], F16)
        gate_lo = sb("gate_lo", [P, KC, E], F16)
        bias_sb = sb("bias_sb", [P, E])
        bnst = sb("bnst", [P, B, 2, 6])
        mv = sb("mv", [P, B, 2])
        msum = sb("msum", [P, B, 2])
        mtmp = sb("mtmp", [P, B])
        mean = sb("mean", [P, B])
        lnvar = sb("lnvar", [P, B])
        rstd = sb("rstd", [P, B])
        smx = sb("smx", [P, 4, 16])
        ssum = sb("ssum", [P, 4, 16])
        sinv = sb("sinv", [P, 4, 16])

        x_res = sb("x_res", [P, NT, D])
        ctx_hi = sb("ctx_hi", [P, KC, T], F16)
        ctx_lo = sb("ctx_lo", [P, KC, T], F16)
        hT_hi = sb("hT_hi", [P, KC, T], F16)
        hT_lo = sb("hT_lo", [P, KC, T], F16)

        reg_x = sb("reg_x", [P, 4096])
        reg_h = sb("reg_h", [P, 4096])
        reg_a = sb("reg_a", [P, 4096])
        reg_b = sb("reg_b", [P, 4096])
        reg_c = sb("reg_c", [P, 4096])
        xh = reg_x[:, :].rearrange("p (n l) -> p n l", n=B)
        hq = reg_h[:, :].rearrange("p (l n) -> p l n", n=B)
        qT1 = reg_a[:, :].rearrange("p (j c) -> p j c", c=P)
        e1 = reg_b[:, 0:2048].rearrange("p (b c) -> p b c", c=BANK)
        p1T = reg_b[:, 2048:4096].rearrange("p (b c) -> p b c", c=BANK)
        ctx_st = reg_c[:, :].rearrange("p (k t) -> p k t", k=KC)
        p1_diag = [w.rearrange("p (j c) -> p j c", c=P) for w in (
            reg_c[:, 0:2048], reg_c[:, 2048:4096],
            hT_hi[:, :, :].rearrange("p k t -> p (k t)").bitcast(F32),
            hT_lo[:, :, :].rearrange("p k t -> p (k t)").bitcast(F32))]
        h2 = reg_h[:, :].rearrange("p (n l) -> p n l", n=B)
        h_tok = reg_h[:, :].rearrange("p (t d) -> p t d", t=NT)

        def halves(region, n=2048):
            return region[:, 0:n].bitcast(F16), region[:, n:2 * n].bitcast(F16)

        q_hi, q_lo = (r.rearrange("p (m b h s) -> p m b h s", m=2, b=B, h=2) for r in halves(reg_a))
        sq_hi, sq_lo = (r.rearrange("p (m b h s) -> p m b h s", m=2, b=B, h=2) for r in halves(reg_c))
        o_hi, o_lo = (r.rearrange("p (h t b s) -> p h t b s", h=HG, t=NT, b=2) for r in halves(reg_b))
        prob = reg_x[:, 0:2048].rearrange("p (b c) -> p b c", c=BANK)
        pT_hi = reg_x[:, 2048:3072].bitcast(F16).rearrange("p (t c) -> p t c", t=NT)
        pT_lo = reg_x[:, 3072:4096].bitcast(F16).rearrange("p (t c) -> p t c", t=NT)

        wq_st = sb("wq_st", [P, KC, BANK])
        wq_hi = sb("wq_hi", [P, KC, BANK], F16)
        wq_lo = sb("wq_lo", [P, KC, BANK], F16)
        wkv_st = sb("wkv_st", [P, KC, 2 * HD])
        wkv_hi = sb("wkv_hi", [P, KC, 2 * HD], F16)
        wkv_lo = sb("wkv_lo", [P, KC, 2 * HD], F16)
        wo_st = sb("wo_st", [P, HG, D])
        wo_hi = sb("wo_hi", [P, HG, D], F16)
        wo_lo = sb("wo_lo", [P, HG, D], F16)
        sq32 = sb("sq32", [P, 2, BANK])
        k32 = sb("k32", [P, 2, BANK])
        ksq32 = sb("ksq32", [P, 2, BANK])
        ksq_hi = sb("ksq_hi", [P, 2, BANK], F16)
        ksq_lo = sb("ksq_lo", [P, 2, BANK], F16)
        rk = sb("rk", [P, 2, BANK])
        k_hi = sb("k_hi", [P, T], F16)
        k_lo = sb("k_lo", [P, T], F16)
        v_hi = sb("v_hi", [P, NT, HD], F16)
        v_lo = sb("v_lo", [P, NT, HD], F16)
        rq = sb("rq", [P, 32])
        rowmax = sb("rowmax", [P, 4, 8])
        rowsum = sb("rowsum", [P, 4, 8])
        rowinv = sb("rowinv", [P, 4, 8])

        def flat(buf):
            return buf[:, :, :].rearrange("p k n -> p (k n)")

        wgu_st = [reg[:, 0:2048].rearrange("p (k n) -> p k n", k=KC) for reg in (reg_c, reg_x)]
        wd_st = [reg[:, 2048:3072].rearrange("p (k n) -> p k n", k=IC) for reg in (reg_c, reg_x)]
        wgu_hi, wgu_lo = (wo_hi, wq_hi), (wo_lo, wq_lo)
        wd_hi = [w.rearrange("p (k n) -> p k n", k=IC) for w in (flat(wkv_hi), reg_x[:, 3072:3584].bitcast(F16))]
        wd_lo = [w.rearrange("p (k n) -> p k n", k=IC) for w in (flat(wkv_lo), reg_x[:, 3584:4096].bitcast(F16))]
        z_hi = reg_a[:, 0:1024].bitcast(F16).rearrange("p (c t) -> p c t", c=IC)
        z_lo = reg_a[:, 1024:2048].bitcast(F16).rearrange("p (c t) -> p c t", c=IC)
        silu = reg_a[:, 2048:3072].rearrange("p (u n) -> p u n", u=2)
        z32 = reg_a[:, 3072:4096].rearrange("p (u n) -> p u n", u=2)
        on_b = reg_b[:, 0:NTK * SW // 2].bitcast(F16).rearrange("p (c s) -> p c s", s=SW)
        on_a = reg_b[:, 2048:2048 + NTK * NS // 2].bitcast(F16).rearrange("p (c s) -> p c s", s=NS)
        on_tok = flat(wq_st)[:, 0:NTK * NS // 2].bitcast(F16).rearrange("p (c s) -> p c s", s=NS)
        def pair(region, col, n, dt=F32):
            words = n if dt == F32 else n // 2
            return [region[:, col + i * words:col + (i + 1) * words].bitcast(dt) if dt != F32 else
                    region[:, col + i * words:col + (i + 1) * words] for i in range(2)]

        tz_hi = [w.rearrange("p (c s) -> p c s", c=IC) for w in pair(reg_b, 0, IC * TS, F16)]
        tz_lo = [w.rearrange("p (c s) -> p c s", c=IC) for w in pair(reg_b, IC * TS, IC * TS, F16)]
        tsilu, tz32 = (w.rearrange("p (c s) -> p c s", c=IC) for w in pair(reg_b, 2 * IC * TS, IC * TS))
        h_slot = [w.rearrange("p (h d) -> p h d", h=2) for w in pair(reg_b, 4 * IC * TS, 2 * HROW)]
        tT_hi = [w.rearrange("p (k s) -> p k s", k=KC) for w in pair(flat(k32), 0, KC * TS, F16)]
        tT_lo = [w.rearrange("p (k s) -> p k s", k=KC) for w in pair(flat(ksq32), 0, KC * TS, F16)]
        y = [w.rearrange("p (h d) -> p h d", h=2) for w in pair(reg_h, 0, 2 * D)]

        score = sb("score", [P, NT, E])
        left = sb("left", [P, NT, E])
        top8 = sb("top8", [P, NT, 8])
        sel = sb("sel", [P, NT, E], F16)
        wsum = sb("wsum", [P, NT])
        cw = sb("cw", [P, NT, E])
        below = sb("below", [P, P], F16)
        row_no = sb("row_no", [P, 1])
        count_up = sb("count_up", [P, P])
        count16 = sb("count16", [P, P], F16)
        tile_steps = sb("tile_steps", [P, NJT])
        hi_steps = sb("hi_steps", [P, HI8])
        lo_steps = sb("lo_steps", [P, HI8 - 1])
        tok_no = sb("tok_no", [P, NT])
        dump_no = sb("dump_no", [P, NS])
        before = sb("before", [P, E, E])
        tiles = sb("tiles", [P, E])
        first_tile = sb("first_tile", [P, E])
        past_tile = sb("past_tile", [P, E])
        eid = sb("eid", [P, TILES])
        eid_int = sb("eid_int", [P, TILES], I32)

        def carve(buf, *widths):
            ends = [sum(widths[:i]) for i in range(len(widths) + 1)]
            return [flat(buf)[:, i:j] for i, j in zip(ends, ends[1:])]

        tile_cmp, steps_cmp, key, key8 = carve(sq32, TILES * E, NTK * HI8, NT * E, NT * 8)
        tile_cmp = tile_cmp.rearrange("p (n e) -> p n e", e=E)
        steps_cmp = steps_cmp.rearrange("p (c j) -> p c j", j=HI8)
        key = key.rearrange("p (t e) -> p t e", e=E)
        key8 = key8.rearrange("p (t k) -> p t k", k=8)
        need, is_eid, slot, slot_hi, slot_lo, slot_rest, dump, row_f = carve(
            rk, E * NJT, TILES * E, NTK, NTK, NTK, NTK, NS, NS)
        slot_a = sb("slot_a", [P, NTK], F16)
        slot_b = sb("slot_b", [P, NTK], F16)
        need = need.rearrange("p (e j) -> p e j", j=NJT)
        is_eid = is_eid.rearrange("p (n e) -> p n e", e=E)
        from_row = sb("from_row", [P, NS], I32)
        to_row = sb("to_row", [P, NS], I32)
        from_now = sb("from_now", [P, 2, 2], I32)
        to_now = sb("to_now", [P, 2, 2], I32)
        cw_cmp = sb("cw_cmp", [P, 2, 2, E])
        cw_slot = sb("cw_slot", [P, 2, 2])

        x_in = [sem(f"x_in{j}") for j in range(4)]
        ctx_in, mask_in, small_in = sem("ctx_in"), sem("mask_in"), sem("small_in")
        wq_in, wkv_in, wo_in = sem("wq_in"), sem("wkv_in"), sem("wo_in")
        wgu_in = [sem(f"wgu_in{i}") for i in range(2)]
        wd_in = [sem(f"wd_in{i}") for i in range(2)]
        zeroed, consts, dve_consts = sem("zeroed"), sem("consts"), sem("dve_consts")
        chain = sem("chain")
        ctx_hi_done, ctx_split = sem("ctx_hi_done"), sem("ctx_split")
        stats1, swapped, var_ready, lnvar_ready, rstd_ready = (
            sem("stats1"), sem("swapped"), sem("var_ready"), sem("lnvar_ready"), sem("rstd_ready"))
        h1_done, x_plus_h = sem("h1_done"), sem("x_plus_h")
        qT1_ps, qT1_done = sem("qT1_ps"), sem("qT1_done")
        gram, s1_shift, e1_done, p1_done = sem("gram"), sem("s1_shift"), sem("e1_done"), sem("p1_done")
        diag_zero, diag_done, h2_done = sem("diag_zero"), sem("diag_done"), sem("h2_done")
        msg, x1_done, x1_moved = sem("msg"), sem("x1_done"), sem("x1_moved")
        h_done, hT_ps, hT_hi_done, hT_split = sem("h_done"), sem("hT_ps"), sem("hT_hi_done"), sem("hT_split")
        wq_hi_done, wq_split = sem("wq_hi_done"), sem("wq_split")
        wkv_hi_done, wkv_split = sem("wkv_hi_done"), sem("wkv_split")
        wo_hi_done, wo_split = sem("wo_hi_done"), sem("wo_split")
        s_ps, q_ps, k_ps, v_ps = sem("s_ps"), sem("q_ps"), sem("k_ps"), sem("v_ps")
        ssq_q_ps, ssq_k_ps, pT_ps, pv_ps, o_ps = (
            sem("ssq_q_ps"), sem("ssq_k_ps"), sem("pT_ps"), sem("pv_ps"), sem("o_ps"))
        q_hi_done, sq32_done, sq_hi_done, sq_split, q_split = (
            sem("q_hi_done"), sem("sq32_done"), sem("sq_hi_done"), sem("sq_split"), sem("q_split"))
        scaled, masked, max_done, shifted, exp_done = (
            sem("scaled"), sem("masked"), sem("max_done"), sem("shifted"), sem("exp_done"))
        sum_done, inv_done, prob_done = sem("sum_done"), sem("inv_done"), sem("prob_done")
        pT_hi_done, pT_split, o_hi_done, o_split = (
            sem("pT_hi_done"), sem("pT_split"), sem("o_hi_done"), sem("o_split"))
        k32_done, ksq32_done, ksq_hi_done, ksq_split = (
            sem("k32_done"), sem("ksq32_done"), sem("ksq_hi_done"), sem("ksq_split"))
        v_hi_done, v_split, k_norm, k_hi_done, k_split = (
            sem("v_hi_done"), sem("v_split"), sem("k_norm"), sem("k_hi_done"), sem("k_split"))
        ln_q, rq_done, ln_k, rk_done, o_added = (
            sem("ln_q"), sem("rq_done"), sem("ln_k"), sem("rk_done"), sem("o_added"))
        gate_hi_done, gate_split, logits, sig_exp, cw_done = (
            sem("gate_hi_done"), sem("gate_split"), sem("logits"), sem("sig_exp"), sem("cw_done"))
        wgu_hi_done, wgu_split, wd_hi_done, wd_split = (
            sem("wgu_hi_done"), sem("wgu_split"), sem("wd_hi_done"), sem("wd_split"))
        gu_ps, silu_done, z32_done, z_hi_done, z_split = (
            sem("gu_ps"), sem("silu_done"), sem("z32_done"), sem("z_hi_done"), sem("z_split"))
        d_ps, d_added, stored = sem("d_ps"), sem("d_added"), sem("stored")
        numbers, tables, h_stored, cw_stored = sem("numbers"), sem("tables"), sem("h_stored"), sem("cw_stored")
        sel_done, rank_ps, eid_done, onehots, slot_ps, rows_done = (
            sem("sel_done"), sem("rank_ps"), sem("eid_done"), sem("onehots"), sem("slot_ps"), sem("rows_done"))
        now, scattered, tokens_set = sem("now"), sem("scattered"), sem("tokens_set")
        gathered = [sem(f"gathered{i}") for i in range(2)]

        tT_ps, tT_hi_done, tT_split, cw_slot_done = sem("tT_ps"), sem("tT_hi_done"), sem("tT_split"), sem("cw_slot_done")
        tgu_ps, tsilu_done, tz32_done, tz_hi_done, tz_split = (
            sem("tgu_ps"), sem("tsilu_done"), sem("tz32_done"), sem("tz_hi_done"), sem("tz_split"))
        cw_cmp_done = sem("cw_cmp_done")
        td_ps, y_done = sem("td_ps"), sem("y_done")

        def loaded(r, par):
            return r * 8 + (8 if par else 16)

        def slots_read(r, par):
            return r * 16 + (16 if par else 0)

        def rounds(eng, step):
            first, last = 4, 4 + (TILES - 3 - 4) // 2 * 2
            for r in range(1, first + 1):
                step(r, r % 2, r)
            with eng.Fori(first // 2, last // 2) as m:
                step(2 * m + 1, 1, first + 1)
                step(2 * m + 2, 0, first + 2)
            for r in range(last + 1, TILES + 1):
                step(r, r % 2, r)

        block = ctx.enter_context(nc.Block())

        @block.sync
        def _(sp):
            xh_d = x_half.rearrange("p (n l) -> p n l", n=B)
            for j in range(4):
                sp.dma_start(xh[:, 4 * j:4 * j + 4, :], xh_d[:, 4 * j:4 * j + 4, :]).then_inc(x_in[j], 16)
            sp.dma_start(ctx_st, ctx_t.rearrange("p (k t) -> p k t", k=KC)).then_inc(ctx_in, 16)
            sp.dma_start(wq_st[:, :, :], wq[0]).then_inc(wq_in, 16)
            sp.dma_start(wkv_st[:, :, :], wkv[0]).then_inc(wkv_in, 16)
            sp.dma_start(wo_st[:, :, :], wo[0]).then_inc(wo_in, 16)
            x_pairs = xh.rearrange("p (t b) l -> p t b l", b=2)
            sp.wait_ge(x1_done, 8)
            for half in range(2):
                for b in range(2):
                    sp.dma_start(x_res[b * S:(b + 1) * S, :, half * HALF:(half + 1) * HALF],
                                 x_pairs[half * S:(half + 1) * S, :, b, :]).then_inc(x1_moved, 16)
            with sp.Fori(1, G) as g:
                sp.wait_ge(wq_split, g * KC)
                sp.dma_start(wq_st[:, :, :], wq[g]).then_inc(wq_in, 16)
                sp.wait_ge(wkv_split, g * 2)
                sp.dma_start(wkv_st[:, :, :], wkv[g]).then_inc(wkv_in, 16)
                sp.wait_ge(wo_split, g * HG)
                sp.dma_start(wo_st[:, :, :], wo[g]).then_inc(wo_in, 16)
            sp.wait_ge(ssq_q_ps, G)
            sp.dma_start(wgu_st[0], wgu[SHARED]).then_inc(wgu_in[0], 16)
            sp.dma_start(wd_st[0], wd[SHARED]).then_inc(wd_in[0], 16)
            rows = h_rows.rearrange("(t p) d -> p t d", p=P)
            sp.wait_ge(h_done, NT)
            sp.dma_start(rows[:, :, 0:D], h_tok).then_inc(h_stored, 16)
            sp.wait_ge(cw_done, 1)
            sp.dma_start(rows[:, :, D:HROW], cw[:, :, :]).then_inc(h_stored, 16)

            def load_expert(n, par):
                e = sp.value_load(eid_int[0:1, bass.ds(n, 1)], min_val=0, max_val=E - 1)
                return (wgu[bass.ds(e, 1), :, :, :].rearrange("o p k n -> p (o k) n"),
                        wd[bass.ds(e, 1), :, :, :].rearrange("o p k n -> p (o k) n"))

            sp.wait_ge(eid_done, 1)
            for r in (1, 2):
                gu_src, d_src = load_expert(r - 1, r % 2)
                if r == 2:
                    sp.wait_ge(wgu_split, KC * (r - 1))
                sp.dma_start(wgu_st[r % 2], gu_src).then_inc(wgu_in[r % 2], 16)
                if r == 2:
                    sp.wait_ge(wd_split, IC * (r - 1))
                sp.dma_start(wd_st[r % 2], d_src).then_inc(wd_in[r % 2], 16)
            for t in range(NT):
                sp.wait_ge(d_added, t + 1)
                sp.dma_start(out[t * P:(t + 1) * P, :], x_res[:, t, :]).then_inc(stored, 16)
            for i in range(2):
                sp.dma_start(out[T + i * SW:T + (i + 1) * SW, :], x_res[0:SW, i, :]).then_inc(stored, 16)
            def load_round(r, par):
                gu_src, d_src = load_expert(r - 1, par)
                sp.wait_ge(wgu_split, (r - 1) * KC)
                sp.dma_start(wgu_st[par], gu_src).then_inc(wgu_in[par], 16)
                sp.wait_ge(wd_split, (r - 1) * IC)
                sp.dma_start(wd_st[par], d_src).then_inc(wd_in[par], 16)

            with sp.Fori(1, TILES // 2) as m:
                load_round(2 * m + 1, 1)
                load_round(2 * m + 2, 0)
            if TILES % 2:
                load_round(TILES, 1)
            sp.wait_ge(scattered, 2 * 16 * TILES)

        @block.gpsimd
        def _(pool):
            pool.memset(ident[:, :], 0.0).then_inc(zeroed, 1)
            pool.memset(swap[:, :], 0.0).then_inc(zeroed, 1)
            pool.memset(blockmask[:, :], 0.0).then_inc(zeroed, 1)
            pool.memset(ones[:, :], 1.0).then_inc(consts, 1)
            pool.memset(eps_ln[:, :], EPS).then_inc(consts, 1)
            pool.memset(eps_q[:, :], 4096.0 * HD * EPS).then_inc(consts, 1)
            pool.wait_ge(zeroed, 3)
            pool.affine_select(out=ident[:, :], in_=ident[:, :], compare_op=ALU.not_equal, fill=1.0,
                               base=0, pattern=[[-1, P]], channel_multiplier=1).then_inc(consts, 1)
            pool.affine_select(out=swap[:, 0:64], in_=swap[:, 0:64], compare_op=ALU.not_equal, fill=1.0,
                               base=-64, pattern=[[-1, 64]], channel_multiplier=1).then_inc(consts, 1)
            pool.affine_select(out=swap[:, 64:128], in_=swap[:, 64:128], compare_op=ALU.not_equal, fill=1.0,
                               base=0, pattern=[[-1, 64]], channel_multiplier=1).then_inc(consts, 1)
            for q in range(4):
                rows = slice(32 * q, 32 * q + 32)
                pool.wait_ge(consts, 6 + 2 * q)
                pool.affine_select(out=blockmask[rows, 0:16], in_=blockmask[rows, 0:16], compare_op=ALU.is_ge,
                                   fill=NEG, base=15, pattern=[[0, 16]], channel_multiplier=-1).then_inc(consts, 1)
                pool.wait_ge(consts, 7 + 2 * q)
                pool.affine_select(out=blockmask[rows, 16:32], in_=blockmask[rows, 16:32], compare_op=ALU.is_ge,
                                   fill=NEG, base=-16, pattern=[[0, 16]], channel_multiplier=1).then_inc(consts, 1)
            pool.wait_ge(consts, 14)

            iotas = [0]

            def iota(buf, pattern, base, per_row):
                if iotas[0]:
                    pool.wait_ge(numbers, iotas[0])
                iotas[0] += 1
                pool.iota(buf, pattern=pattern, base=base, channel_multiplier=per_row,
                          allow_small_or_imprecise_dtypes=True).then_inc(numbers, 1)

            iota(count_up[:, :], [[1, P]], 0, 0)
            iota(row_no[:, :], [[1, 1]], 0, 1)
            iota(tile_steps[:, :], [[TS, NJT]], 0, 0)
            iota(hi_steps[:, :], [[HI8 * SW, HI8]], HI8 * SW, 0)
            iota(lo_steps[:, :], [[SW, HI8 - 1]], SW, 0)
            iota(tok_no[:, :], [[P, NT]], -T, 1)
            iota(dump_no[:, :], [[0, TILES], [SW, 2]], 0, 1)
            pool.wait_ge(numbers, 7)
            pool.memset(p1_diag[2], 0.0).then_inc(diag_zero, 1)
            pool.wait_ge(diag_zero, 1)
            pool.memset(p1_diag[3], 0.0).then_inc(diag_zero, 1)
            pool.wait_ge(diag_zero, 2)
            for c in range(KC):
                pool.wait_ge(ctx_hi_done, c + 1)
                pool.tensor_tensor(ctx_lo[:, c, :], ctx_st[:, c, :], ctx_hi[:, c, :],
                                   ALU.subtract).then_inc(ctx_split, 1)
            pool.wait_ge(ctx_split, KC)
            pool.memset(reg_c[:, :], 0.0).then_inc(diag_zero, 2)
            pool.wait_ge(diag_zero, 4)
            pool.wait_ge(h1_done, B)
            for j in range(4):
                n = slice(4 * j, 4 * j + 4)
                pool.tensor_tensor(xh[:, n, :], xh[:, n, :], hq[:, :, n].rearrange("p l n -> p n l"),
                                   ALU.add).then_inc(x_plus_h, 1)

            def mask_add(i, b):
                pool.wait_ge(scaled, ev(i, 4, b))
                t = prob[:, b, :].rearrange("p (g k) -> p g k", k=S)
                pool.tensor_tensor(t, t, mask_sb[:, :].unsqueeze(1).to_broadcast([P, 8, S]),
                                   ALU.add).then_inc(masked, 1)

            def shift(i, b):
                pool.wait_ge(max_done, ev(i, 4, b))
                t = prob[:, b, :].rearrange("p (g k) -> p g k", k=S)
                pool.tensor_tensor(t, t, rowmax[:, b, :].unsqueeze(2).to_broadcast([P, 8, S]),
                                   ALU.subtract).then_inc(shifted, 1)

            def square_lo(p, u):
                j, th = u // 2, u % 2
                pool.wait_ge(sq_hi_done, ev(p, 8, u))
                w = sq_hi[:, j // 2, 8 * th:8 * th + 8, j % 2, :]
                pool.tensor_tensor(sq_lo[:, j // 2, 8 * th:8 * th + 8, j % 2, :],
                                   sq32[:, u % 2, :].rearrange("p (b s) -> p b s", s=S), w,
                                   ALU.subtract).then_inc(sq_split, 1)

            def k_square_lo(p, th):
                pool.wait_ge(ksq_hi_done, ev(p, 2, th))
                pool.tensor_tensor(ksq_lo[:, th, :], ksq32[:, th, :], ksq_hi[:, th, :],
                                   ALU.subtract).then_inc(ksq_split, 1)

            def iteration(i, att, proj):
                if att and proj:
                    for b in range(4):
                        mask_add(i, b)
                for k in range(8):
                    if att and not proj and k < 4:
                        mask_add(i, k)
                    if att and proj and k < 4:
                        shift(i, k)
                    if att and not proj and 1 <= k < 5:
                        shift(i, k - 1)
                    if proj:
                        square_lo(i + 1, k)
                if proj and att:
                    k_square_lo(i + 1, 0)
                    k_square_lo(i + 1, 1)

            k_square_lo(0, 0)
            k_square_lo(0, 1)
            iteration(-1, False, True)
            pool.wait_ge(mask_in, 32)
            with pool.Fori(0, G - 1) as i:
                iteration(i, True, True)
            iteration(G - 1, True, False)

            for u in range(4):
                pool.wait_ge(z_hi_done, u + 1)
                c, th = u % 2, u // 2
                cols = slice(th * BANK, th * BANK + BANK)
                pool.tensor_tensor(z_lo[:, c, cols], z32[:, u % 2, :], z_hi[:, c, cols],
                                   ALU.subtract).then_inc(z_split, 1)

            def gather(r, par, copies):
                pool.tensor_copy(from_now[0:SW, par, :], from_row[0:SW, bass.ds((r - 1) * 2, 2)]).then_inc(now, 1)
                pool.wait_ge(now, copies)
                pool.nop(nofuse=True)
                for h in range(2):
                    pool.indirect_dma_start(h_slot[par][0:SW, h, :], None, h_rows, bass.IndirectOffsetOnAxis(
                        ap=from_now[0:SW, par, h:h + 1], axis=0)).then_inc(gathered[par], 16)

            def scatter(r, par, n, copies):
                pool.wait_ge(y_done, 2 * r)
                if n >= 2:
                    pool.wait_ge(scattered, 32 * (r - 1))
                pool.nop(nofuse=True)
                pool.tensor_copy(to_now[0:SW, par, :], to_row[0:SW, bass.ds((r - 1) * 2, 2)]).then_inc(now, 1)
                pool.wait_ge(now, copies)
                if n == 1:
                    pool.wait_ge(stored, 16 * (NT + 2))
                pool.nop(nofuse=True)
                for h in range(2):
                    pool.indirect_dma_start(out, bass.IndirectOffsetOnAxis(ap=to_now[0:SW, par, h:h + 1], axis=0),
                                            y[par][0:SW, h, :], None, compute_op=ALU.add).then_inc(scattered, 16)

            def step(r, par, n):
                ahead = r + 3
                if n <= TILES - 3:
                    pool.wait_ge(tT_ps, 2 * r + 2)
                    pool.wait_ge(cw_cmp_done, r + 1)
                    pool.nop(nofuse=True)
                    gather(ahead, 1 - par, ahead + (r - 3 if n >= 3 else 0))
                else:
                    ahead = TILES
                if n >= 3:
                    scatter(r - 2, par, n - 2, ahead + r - 2)
                for c in range(IC):
                    pool.wait_ge(tz_hi_done, 2 * (r - 1) + c + 1)
                    pool.tensor_tensor(tz_lo[par][:, c, :], tz32[:, c, :], tz_hi[par][:, c, :],
                                       ALU.subtract).then_inc(tz_split, 1)

            pool.wait_ge(rows_done, 1)
            pool.wait_ge(h_stored, 32)
            for r in (1, 2, 3):
                if r == 3:
                    pool.wait_ge(tT_ps, 2)
                    pool.wait_ge(cw_cmp_done, 1)
                gather(r, r % 2, r)
            rounds(pool, step)
            for r in (TILES - 1, TILES):
                scatter(r, r % 2, r, TILES + r)

        @block.scalar
        def _(act):
            act.preload_act_table_set("natural_log_exp_and_others")
            act.dma_start(mask_sb[0:S, :], mask).then_inc(mask_in, 16)
            act.dma_start(mask_sb[S:P, :], mask).then_inc(mask_in, 16)
            act.dma_start(norm_sb[:, :], qk_norm).then_inc(small_in, 16)
            act.dma_start(gate_st[:, :, :], gate_t.rearrange("p (k e) -> p k e", k=KC)).then_inc(small_in, 16)
            act.dma_start(bias_sb[:, :], bias).then_inc(small_in, 16)

            def ln_rstd(count, n):
                act.wait_ge(var_ready, count)
                act.activation(lnvar[:, n], lnvar[:, n], ACT.Ln, bias=eps_ln[:, :]).then_inc(lnvar_ready, 1)
                act.wait_ge(lnvar_ready, count)
                act.activation(rstd[:, n], lnvar[:, n], ACT.Exp, scale=-0.5).then_inc(rstd_ready, 1)

            act.wait_ge(consts, 14)
            ln_rstd(1, slice(0, B))
            act.wait_ge(ctx_in, 16)
            for c in range(KC):
                act.activation(ctx_hi[:, c, :], ctx_st[:, c, :], ACT.Copy).then_inc(ctx_hi_done, 1)
            def wq_chunk(c, first=False):
                act.activation(wq_hi[:, c, :], wq_st[:, c, :], ACT.Copy, scale=WS).then_inc(wq_hi_done, 1)

            def wkv_chunk(c):
                act.activation(wkv_hi[:, 2 * c:2 * c + 2, :], wkv_st[:, 2 * c:2 * c + 2, :], ACT.Copy,
                               scale=WS).then_inc(wkv_hi_done, 1)

            def first_exp(b):
                act.wait_ge(s1_shift, b + 1)
                act.activation(e1[:, b, :], e1[:, b, :], ACT.Exp, scale=float(S) ** -0.5).then_inc(e1_done, 1)

            def first_qT(t):
                act.wait_ge(qT1_ps, t + 1)
                act.activation(qT1[:, 4 * t:4 * t + 4, :], ps[:, 4 + t % 4, :].rearrange("p (j c) -> p j c", c=P),
                               ACT.Copy).then_inc(qT1_done, 1)

            def first_diag(b):
                act.wait_ge(p1_done, b + 1)
                act.wait_ge(diag_zero, 4)
                for k in range(4):
                    rows = slice(32 * k, 32 * k + 32)
                    act.activation(p1_diag[b][rows, :, rows], p1T[rows, b, :].rearrange("p (j m) -> p j m", m=32),
                                   ACT.Copy).then_inc(diag_done, 1)

            for t in range(8):
                first_qT(t)
            first_exp(0)
            for b in range(1, 4):
                first_exp(b)
                first_diag(b - 1)
            first_diag(3)
            act.wait_ge(wkv_in, 16)
            for c in range(2):
                wkv_chunk(c)
            act.wait_ge(wq_in, 16)
            for c in range(KC):
                wq_chunk(c)
            act.wait_ge(small_in, 48)
            act.activation(gate_hi[:, :, :], gate_st[:, :, :], ACT.Copy, scale=WS).then_inc(gate_hi_done, 1)

            def transposed_hi(base, t, bank):
                act.wait_ge(hT_ps, base + t + 1)
                act.activation(hT_hi[:, :, t * P:(t + 1) * P], ps[:, bank, :].rearrange("p (k c) -> p k c", c=P),
                               ACT.Copy).then_inc(hT_hi_done, 1)

            def q_parts(p, u):
                j, th = u // 2, u % 2
                bank = ps[:, 4 + u % 2, :]
                act.wait_ge(q_ps, ev(p, 8, u))
                act.activation(q_hi[:, j // 2, 8 * th:8 * th + 8, j % 2, :],
                               bank.rearrange("p (b s) -> p b s", s=S), ACT.Copy).then_inc(q_hi_done, 1)
                if u >= 2:
                    act.wait_ge(sq_split, ev(p, 8, u - 2))
                act.activation(sq32[:, u % 2, :], bank, ACT.Square, scale=4.0 / WS).then_inc(sq32_done, 1)
                act.wait_ge(sq32_done, ev(p, 8, u))
                act.activation(sq_hi[:, j // 2, 8 * th:8 * th + 8, j % 2, :],
                               sq32[:, u % 2, :].rearrange("p (b s) -> p b s", s=S),
                               ACT.Copy).then_inc(sq_hi_done, 1)

            def soft_exp(i, b):
                act.wait_ge(shifted, ev(i, 4, b))
                act.activation(prob[:, b, :], prob[:, b, :], ACT.Exp).then_inc(exp_done, 1)

            def probs_hi(i, t):
                act.wait_ge(pT_ps, ev(i, NT, t))
                act.activation(pT_hi[:, t, :], ps[:, 6 + t % 2, 0:256], ACT.Copy).then_inc(pT_hi_done, 1)

            def heads_hi(i, t):
                act.wait_ge(pv_ps, ev(i, NT, t))
                act.activation(o_hi[:, :, t, :, :].rearrange("p h b s -> p b h s"),
                               ps[:, 0:2, 0:256].rearrange("p b (h s) -> p b h s", s=S),
                               ACT.Copy).then_inc(o_hi_done, 1)

            def k_parts(p, th):
                act.wait_ge(k_ps, ev(p, 2, th))
                act.activation(k32[:, th, :], ps[:, 4 + th, :], ACT.Copy, scale=1.0 / WS).then_inc(k32_done, 1)
                act.activation(ksq32[:, th, :], ps[:, 4 + th, :], ACT.Square, scale=4.0 / WS).then_inc(ksq32_done, 1)
                act.wait_ge(ksq32_done, ev(p, 2, th))
                act.activation(ksq_hi[:, th, :], ksq32[:, th, :], ACT.Copy).then_inc(ksq_hi_done, 1)

            def k_scale(p, th):
                act.wait_ge(ssq_k_ps, ev(p, 2, th))
                act.activation(rk[:, th, :], ps[:, 4 + th, :], ACT.Ln, scale=1.0 / (16 * HD),
                               bias=eps_ln[:, :]).then_inc(ln_k, 1)
                act.wait_ge(ln_k, ev(p, 2, th))
                act.activation(rk[:, th, :], rk[:, th, :], ACT.Exp, scale=-0.5).then_inc(rk_done, 1)

            def k_hi_part(p, th):
                act.wait_ge(k_norm, ev(p, 2, th))
                act.activation(k_hi[:, th * BANK:(th + 1) * BANK], k32[:, th, :], ACT.Copy).then_inc(k_hi_done, 1)

            def q_rms(p):
                act.wait_ge(ssq_q_ps, p + 1)
                act.activation(rq[:, :], ps[:, 3, 0:32], ACT.Ln, scale=WS * WS / 16, bias=eps_q[:, :]).then_inc(ln_q, 1)
                act.wait_ge(ln_q, p + 1)
                act.activation(rq[:, :], rq[:, :], ACT.Exp, scale=-0.5).then_inc(rq_done, 1)

            def v_hi_part(p, th, bank):
                act.wait_ge(v_ps, ev(p, 2, th))
                act.activation(v_hi[:, 4 * th:4 * th + 4, :], ps[:, bank, :].rearrange("p (t d) -> p t d", d=HD),
                               ACT.Copy).then_inc(v_hi_done, 1)

            def expert_weights_hi(r, par, c):
                if c == 0:
                    act.wait_ge(wgu_in[par], loaded(r, par))
                act.activation(wgu_hi[par][:, c, :], wgu_st[par][:, c, :], ACT.Copy, scale=WS).then_inc(wgu_hi_done, 1)

            def down_weights_hi(r, par, c):
                if c == 0:
                    act.wait_ge(wd_in[par], loaded(r, par))
                act.activation(wd_hi[par][:, c, :], wd_st[par][:, c, :], ACT.Copy, scale=WS).then_inc(wd_hi_done, 1)

            def out_weights_hi(i, c, hi):
                if c == 0:
                    act.wait_ge(wo_in, 16 * i + 16)
                act.activation(hi[:, c, :], wo_st[:, c, :], ACT.Copy, scale=WS).then_inc(wo_hi_done, 1)

            def iteration(i, att, proj, split):
                p = i + 1
                for k in range(8):
                    if proj:
                        q_parts(p, k)
                    if att and 1 <= k < 5:
                        soft_exp(i, k - 1)
                    if att and proj and k >= 4:
                        out_weights_hi(i, k - 4, wo_hi)
                    if att and not proj and k == 2:
                        probs_hi(i, 0)
                        probs_hi(i, 1)
                    if att and not proj and k == 3:
                        heads_hi(i, 0)
                if att and proj:
                    k_parts(p, 0)
                    probs_hi(i, 0)
                    probs_hi(i, 1)
                    k_parts(p, 1)
                    heads_hi(i, 0)
                if proj:
                    q_rms(p)
                if att and proj:
                    k_scale(p, 0)
                for t in range(NT if att or split else 0):
                    if att and t + 2 < NT:
                        probs_hi(i, t + 2)
                    if split and t < KC:
                        if t == 0:
                            act.wait_ge(wq_in, 16 * (i + 3))
                        wq_chunk(t)
                    if att and proj and not split and t < HG:
                        out_weights_hi(G - 1, t, wq_hi)
                    if att and proj and t in (3, 4):
                        k_hi_part(p, t - 3)
                    if not proj and t < KC:
                        expert_weights_hi(0, 0, t)
                    if not proj and KC <= t < KC + IC:
                        down_weights_hi(0, 0, t - KC)
                    if att and t + 1 < NT:
                        heads_hi(i, t + 1)
                    if att and proj and t == 0:
                        k_scale(p, 1)
                    if att and proj and t >= 6:
                        v_hi_part(p, t - 6, t - 2)
                    if not proj and t >= 1:
                        third_norm(t - 1)
                    if not proj and t >= 3:
                        transposed_hi(NT, t - 3, 4 + (t - 3) % 2)
                if split:
                    act.wait_ge(wkv_in, 16 * (i + 3))
                    wkv_chunk(0)
                    wkv_chunk(1)

            def third_norm(t):
                ln_rstd(3 + t, slice(t, t + 1))

            k_parts(0, 0)
            k_parts(0, 1)
            ln_rstd(2, slice(0, B))
            v_hi_part(0, 0, 6)
            for t in range(2):
                transposed_hi(0, t, t % 4)
            v_hi_part(0, 1, 7)
            k_scale(0, 0)
            for t in range(2, 5):
                transposed_hi(0, t, t % 4)
            k_scale(0, 1)
            for t in range(5, NT):
                transposed_hi(0, t, t % 4)
            k_hi_part(0, 0)
            k_hi_part(0, 1)
            iteration(-1, False, True, True)
            with act.Fori(0, G - 2) as i:
                iteration(i, True, True, True)
            iteration(G - 2, True, True, False)
            iteration(G - 1, True, False, False)
            third_norm(NT - 1)
            for t in range(NT - 3, NT):
                transposed_hi(NT, t, 4 + t % 2)

            act.wait_ge(logits, 1)
            act.activation(score[:, :, :], ps[:, 7, 0:NT * E].rearrange("p (t e) -> p t e", e=E), ACT.Exp,
                           scale=-1.0 / WS).then_inc(sig_exp, 1)

            def z_hi_part(u):
                act.wait_ge(z32_done, u + 1)
                c, th = u % 2, u // 2
                act.activation(z_hi[:, c, th * BANK:(th + 1) * BANK], z32[:, u % 2, :], ACT.Copy).then_inc(z_hi_done, 1)

            for u in range(4):
                act.wait_ge(gu_ps, u + 1)
                if u >= 2:
                    act.wait_ge(z32_done, u - 1)
                act.activation(silu[:, u % 2, :], ps[:, 2 * (u % 3), :], ACT.Silu, scale=1.0 / WS).then_inc(silu_done, 1)
                if u >= 1:
                    z_hi_part(u - 1)
            act.wait_ge(onehots, 1)
            for t in range(NT):
                ks = slice(t * TOPK, (t + 1) * TOPK)
                act.activation(on_tok[:, ks, :], on_a[:, ks, :], ACT.Copy, scale=tok_no[:, t:t + 1]).then_inc(tokens_set, 1)
            z_hi_part(3)

            def slots_hi(r, par):
                for j in range(2):
                    act.wait_ge(tT_ps, 2 * (r - 1) + j + 1)
                    act.activation(tT_hi[par][:, 2 * j:2 * j + 2, :],
                                   ps[:, 4 + j, 0:2 * TS].rearrange("p (k s) -> p k s", k=2),
                                   ACT.Copy).then_inc(tT_hi_done, 1)

            def gated(r, c):
                act.wait_ge(tgu_ps, 2 * (r - 1) + c + 1)
                act.activation(tsilu[:, c, :], ps[:, c, 0:TS], ACT.Silu, scale=1.0 / WS).then_inc(tsilu_done, 1)

            def gated_hi(r, par, c):
                act.wait_ge(tz32_done, 2 * (r - 1) + c + 1)
                act.activation(tz_hi[par][:, c, :], tz32[:, c, :], ACT.Copy).then_inc(tz_hi_done, 1)

            def weighted(r, par, n, h):
                act.wait_ge(td_ps, 2 * (r - 1) + h + 1)
                if h == 0:
                    act.wait_ge(cw_slot_done, r)
                    if n >= 3:
                        act.wait_ge(scattered, 32 * (r - 2))
                act.activation(y[par][0:SW, h, :], ps[0:SW, 6 + h, :], ACT.Copy,
                               scale=cw_slot[0:SW, par, h:h + 1]).then_inc(y_done, 1)

            def step(r, par, n):
                more = n < TILES
                if more:
                    slots_hi(r + 1, 1 - par)
                    if n == 1:
                        act.wait_ge(gu_ps, 4)
                    else:
                        act.wait_ge(tgu_ps, 2 * (r - 1))
                    expert_weights_hi(r + 1, 1 - par, 0)
                    expert_weights_hi(r + 1, 1 - par, 1)
                gated(r, 0)
                if more:
                    expert_weights_hi(r + 1, 1 - par, 2)
                gated_hi(r, par, 0)
                if more:
                    expert_weights_hi(r + 1, 1 - par, 3)
                gated(r, 1)
                down_weights_hi(r, par, 0)
                gated_hi(r, par, 1)
                down_weights_hi(r, par, 1)
                if n >= 2:
                    for h in range(2):
                        weighted(r - 1, 1 - par, n - 1, h)

            for c in range(KC):
                expert_weights_hi(1, 1, c)
            slots_hi(1, 1)
            rounds(act, step)
            for h in range(2):
                weighted(TILES, TILES % 2, TILES, h)

        @block.vector
        def _(dve):
            steps = [0]

            def then(ins):
                steps[0] += 1
                ins.then_inc(chain, 1)
                dve.wait_ge(chain, steps[0])

            def half_rows(n):
                return dve.bn_stats(bnst[:, n, 0, :], xh[:, n, :])

            def joined(parts):
                for n in range(B):
                    last = dve.bn_aggr(mv[:, n, :], bnst[:, n, 0:parts, :])
                last.then_inc(stats1, 1)

            def row_scales(count, bank):
                dve.wait_ge(stats1, count)
                dve.wait_ge(swapped, count)
                other = ps[:, bank, 0:2 * B].rearrange("p (n s) -> p n s", s=2)
                dve.tensor_tensor(msum[:, :, :], mv[:, :, :], other, ALU.add)
                then(dve.tensor_tensor(mtmp[:, :], mv[:, :, 0], other[:, :, 0], ALU.subtract))
                then(dve.tensor_tensor(mtmp[:, :], mtmp[:, :], mtmp[:, :], ALU.mult))
                then(dve.scalar_tensor_tensor(lnvar[:, :], mtmp[:, :], 0.5, msum[:, :, 1], ALU.mult, ALU.add))
                dve.tensor_scalar(mean[:, :], msum[:, :, 0], 0.5, None, ALU.mult)
                dve.tensor_scalar(lnvar[:, :], lnvar[:, :], 0.5, None, ALU.mult).then_inc(var_ready, 1)

            for j in range(4):
                dve.wait_ge(x_in[j], 16)
                for n in range(4 * j, 4 * j + 4):
                    last = half_rows(n)
                then(last)
            joined(1)
            row_scales(1, 7)
            dve.wait_ge(rstd_ready, 1)
            for n in range(B):
                dve.tensor_scalar(hq[:, :, n], xh[:, n, :], mean[:, n:n + 1], rstd[:, n:n + 1],
                                  ALU.subtract, ALU.mult).then_inc(h1_done, 1)

            def wq_lo_chunk(c):
                dve.scalar_tensor_tensor(wq_lo[:, c, :], wq_st[:, c, :], WS, wq_hi[:, c, :],
                                         ALU.mult, ALU.subtract).then_inc(wq_split, 1)

            def wkv_lo_chunk(c):
                dve.scalar_tensor_tensor(wkv_lo[:, 2 * c:2 * c + 2, :], wkv_st[:, 2 * c:2 * c + 2, :], WS,
                                         wkv_hi[:, 2 * c:2 * c + 2, :], ALU.mult, ALU.subtract).then_inc(wkv_split, 1)

            def first_shift(b):
                dve.wait_ge(gram, b + 1)
                blocks = e1[:, b, :].rearrange("p (j m) -> p j m", m=32)
                then(dve.tensor_tensor(blocks, ps[:, b, :].rearrange("p (j m) -> p j m", m=32),
                                       blockmask[:, :].unsqueeze(1).to_broadcast([P, 16, 32]), ALU.add))
                then(dve.tensor_reduce(smx[:, b, :], blocks, AX.X, ALU.max))
                dve.tensor_tensor(blocks, blocks, smx[:, b, :].unsqueeze(2).to_broadcast([P, 16, 32]),
                                  ALU.subtract).then_inc(s1_shift, 1)

            def first_probs(b):
                blocks = e1[:, b, :].rearrange("p (j m) -> p j m", m=32)
                dve.wait_ge(e1_done, b + 1)
                then(dve.tensor_reduce(ssum[:, b, :], blocks, AX.X, ALU.add))
                then(dve.reciprocal(sinv[:, b, :], ssum[:, b, :]))
                then(dve.tensor_tensor(blocks, blocks, sinv[:, b, :].unsqueeze(2).to_broadcast([P, 16, 32]), ALU.mult))
                dve.transpose(p1T[:, b, :], e1[:, b, :]).then_inc(p1_done, 1)

            dve.wait_ge(numbers, 7)
            dve.tensor_copy(count16[:, :], count_up[:, :])
            dve.tensor_scalar(below[:, :], count_up[:, :], row_no[:, 0:1], None, ALU.is_gt)
            dve.tensor_tensor(before[:, :, :], count_up[:, 0:E].unsqueeze(1).to_broadcast([P, E, E]),
                              count_up[:, 0:E].unsqueeze(2).to_broadcast([P, E, E]), ALU.is_lt)

            first_shift(0)
            for b in range(1, 4):
                first_shift(b)
                first_probs(b - 1)
            first_probs(3)
            dve.wait_ge(x_plus_h, 4)
            xl = xh.rearrange("p n l -> p l n")
            for u in range(8):
                dve.wait_ge(msg, u + 1)
                part = xl[:, 32 * u:32 * u + 32, :]
                dve.tensor_tensor(part, part, ps[:, (u + 4) % 8, :].rearrange("p (l n) -> p l n", n=B),
                                  ALU.add).then_inc(x1_done, 1)
                if u == 3:
                    for c in range(2):
                        dve.wait_ge(wkv_hi_done, c + 1)
                        wkv_lo_chunk(c)
                    dve.wait_ge(x1_done, 4)
                    for n in range(B):
                        last = dve.bn_stats(bnst[:, n, 0, :], xh[:, n, 0:P])
            dve.wait_ge(x1_done, 8)
            for n in range(B):
                last = dve.bn_stats(bnst[:, n, 1, :], xh[:, n, P:2 * P])
            then(last)
            joined(2)

            def transposed_lo(base, t, bank):
                dve.wait_ge(hT_hi_done, base + t + 1)
                dve.tensor_tensor(hT_lo[:, :, t * P:(t + 1) * P], ps[:, bank, :].rearrange("p (k c) -> p k c", c=P),
                                  hT_hi[:, :, t * P:(t + 1) * P], ALU.subtract).then_inc(hT_split, 1)

            def v_lo_part(p, th, bank):
                dve.wait_ge(v_hi_done, ev(p, 2, th))
                dve.tensor_tensor(v_lo[:, 4 * th:4 * th + 4, :], ps[:, bank, :].rearrange("p (t d) -> p t d", d=HD),
                                  v_hi[:, 4 * th:4 * th + 4, :], ALU.subtract).then_inc(v_split, 1)

            for c in range(KC):
                dve.wait_ge(wq_hi_done, c + 1)
                wq_lo_chunk(c)
            dve.wait_ge(gate_hi_done, 1)
            dve.scalar_tensor_tensor(gate_lo[:, :, :], gate_st[:, :, :], WS, gate_hi[:, :, :],
                                     ALU.mult, ALU.subtract).then_inc(gate_split, 1)
            dve.wait_ge(small_in, 48)
            dve.tensor_tensor(wqk[:, :], norm_sb[:, 0:1], norm_sb[:, 1:2], ALU.mult).then_inc(dve_consts, 1)
            row_scales(2, 0)
            dve.wait_ge(rstd_ready, 2)
            for n in range(B):
                dve.tensor_scalar(h2[:, n, :], xh[:, n, :], mean[:, n:n + 1], rstd[:, n:n + 1],
                                  ALU.subtract, ALU.mult).then_inc(h2_done, 1)
            for t in range(NT):
                transposed_lo(0, t, t % 4)
            v_lo_part(0, 0, 6)
            v_lo_part(0, 1, 7)

            def q_lo_part(p, u):
                j, th = u // 2, u % 2
                dve.wait_ge(q_hi_done, ev(p, 8, u))
                dve.wait_ge(sq32_done, ev(p, 8, u))
                dve.tensor_tensor(q_lo[:, j // 2, 8 * th:8 * th + 8, j % 2, :],
                                  ps[:, 4 + u % 2, :].rearrange("p (b s) -> p b s", s=S),
                                  q_hi[:, j // 2, 8 * th:8 * th + 8, j % 2, :], ALU.subtract).then_inc(q_split, 1)

            def scale_scores(i, b):
                dve.wait_ge(s_ps, ev(i, 4, b))
                if b == 0:
                    dve.wait_ge(rq_done, i + 1)
                dve.tensor_tensor(prob[:, b, :].rearrange("p (g k) -> p g k", k=S),
                                  ps[:, b, :].rearrange("p (g k) -> p g k", k=S),
                                  rq[:, 8 * b:8 * b + 8].unsqueeze(2).to_broadcast([P, 8, S]),
                                  ALU.mult).then_inc(scaled, 1)

            def row_max(i, b):
                dve.wait_ge(masked, ev(i, 4, b))
                dve.tensor_reduce(rowmax[:, b, :], prob[:, b, :].rearrange("p (g k) -> p g k", k=S),
                                  AX.X, ALU.max).then_inc(max_done, 1)

            def normalise(i, b):
                t = prob[:, b, :].rearrange("p (g k) -> p g k", k=S)
                dve.wait_ge(exp_done, ev(i, 4, b))
                dve.tensor_reduce(rowsum[:, b, :], t, AX.X, ALU.add).then_inc(sum_done, 1)
                dve.wait_ge(sum_done, ev(i, 4, b))
                dve.reciprocal(rowinv[:, b, :], rowsum[:, b, :]).then_inc(inv_done, 1)
                dve.wait_ge(inv_done, ev(i, 4, b))
                dve.tensor_tensor(t, t, rowinv[:, b, :].unsqueeze(2).to_broadcast([P, 8, S]),
                                  ALU.mult).then_inc(prob_done, 1)

            def probs_lo(i, t):
                dve.wait_ge(pT_hi_done, ev(i, NT, t))
                dve.tensor_tensor(pT_lo[:, t, :], ps[:, 6 + t % 2, 0:256], pT_hi[:, t, :],
                                  ALU.subtract).then_inc(pT_split, 1)

            def heads_lo(i, t):
                dve.wait_ge(o_hi_done, ev(i, NT, t))
                dve.tensor_tensor(o_lo[:, :, t, :, :].rearrange("p h b s -> p b h s"),
                                  ps[:, 0:2, 0:256].rearrange("p b (h s) -> p b h s", s=S),
                                  o_hi[:, :, t, :, :].rearrange("p h b s -> p b h s"),
                                  ALU.subtract).then_inc(o_split, 1)

            def add_output(i, t):
                dve.wait_ge(o_ps, ev(i, NT, t))
                dve.scalar_tensor_tensor(x_res[:, t, :], ps[:, 2 + t % 2, :], 1.0 / (WS * WS), x_res[:, t, :],
                                         ALU.mult, ALU.add).then_inc(o_added, 1)

            def key_norm(p, th):
                dve.wait_ge(rk_done, ev(p, 2, th))
                dve.wait_ge(k32_done, ev(p, 2, th))
                if th == 0:
                    dve.wait_ge(dve_consts, 1)
                dve.scalar_tensor_tensor(k32[:, th, :], k32[:, th, :], wqk[:, 0:1], rk[:, th, :],
                                         ALU.mult, ALU.mult).then_inc(k_norm, 1)

            def key_lo(p, th):
                cols = slice(th * BANK, (th + 1) * BANK)
                dve.wait_ge(k_hi_done, ev(p, 2, th))
                dve.tensor_tensor(k_lo[:, cols], k32[:, th, :], k_hi[:, cols], ALU.subtract).then_inc(k_split, 1)

            def expert_weights_lo(r, par, c):
                dve.wait_ge(wgu_hi_done, KC * r + c + 1)
                dve.scalar_tensor_tensor(wgu_lo[par][:, c, :], wgu_st[par][:, c, :], WS, wgu_hi[par][:, c, :],
                                         ALU.mult, ALU.subtract).then_inc(wgu_split, 1)

            def down_weights_lo(r, par, c):
                dve.wait_ge(wd_hi_done, IC * r + c + 1)
                dve.scalar_tensor_tensor(wd_lo[par][:, c, :], wd_st[par][:, c, :], WS, wd_hi[par][:, c, :],
                                         ALU.mult, ALU.subtract).then_inc(wd_split, 1)

            def third_stats(t):
                dve.wait_ge(o_added, ev(G - 1, NT, t))
                then(dve.bn_stats(bnst[:, t, 0, :], x_res[:, t, :]))
                then(dve.bn_aggr(mv[:, t, :], bnst[:, t, 0:1, :]))
                dve.tensor_copy(lnvar[:, t:t + 1], mv[:, t, 1:2]).then_inc(var_ready, 1)

            def third_norm(t):
                dve.wait_ge(rstd_ready, 3 + t)
                dve.tensor_scalar(h_tok[:, t, :], x_res[:, t, :], mv[:, t, 0:1], rstd[:, t:t + 1],
                                  ALU.subtract, ALU.mult).then_inc(h_done, 1)

            def out_weights_lo(i, c, hi, lo):
                dve.wait_ge(wo_hi_done, ev(i, HG, c))
                dve.scalar_tensor_tensor(lo[:, c, :], wo_st[:, c, :], WS, hi[:, c, :],
                                         ALU.mult, ALU.subtract).then_inc(wo_split, 1)

            def iteration(i, att, proj, split):
                p = i + 1
                if att and proj:
                    for b in range(4):
                        scale_scores(i, b)
                for k in range(8 if proj else 0):
                    if att and k < 2:
                        row_max(i, 2 * k)
                        row_max(i, 2 * k + 1)
                    q_lo_part(p, k)
                    if att and 2 <= k < 6:
                        normalise(i, k - 2)
                    if att and k >= 4:
                        out_weights_lo(i, k - 4, wo_hi, wo_lo)
                if not proj:
                    scale_scores(i, 0)
                    scale_scores(i, 1)
                    row_max(i, 0)
                    scale_scores(i, 2)
                    row_max(i, 1)
                    normalise(i, 0)
                    scale_scores(i, 3)
                    row_max(i, 2)
                    probs_lo(i, 0)
                    probs_lo(i, 1)
                    normalise(i, 1)
                    row_max(i, 3)
                    heads_lo(i, 0)
                    normalise(i, 2)
                elif att:
                    probs_lo(i, 0)
                    probs_lo(i, 1)
                    heads_lo(i, 0)
                for t in range(NT if att or split else 0):
                    if att and t >= 1:
                        add_output(i, t - 1)
                        if not proj:
                            third_stats(t - 1)
                    if att and t + 2 < NT:
                        probs_lo(i, t + 2)
                    if not proj and t == 0:
                        normalise(i, 3)
                    if att and proj and t in (1, 2):
                        key_norm(p, t - 1)
                    if split and 2 <= t < 2 + KC:
                        dve.wait_ge(wq_hi_done, ev(i + 2, KC, t - 2))
                        wq_lo_chunk(t - 2)
                    if att and proj and not split and 2 <= t < 2 + HG:
                        out_weights_lo(G - 1, t - 2, wq_hi, wq_lo)
                    if att and proj and t in (5, 6):
                        key_lo(p, t - 5)
                    if not proj and 1 <= t < 1 + KC:
                        expert_weights_lo(0, 0, t - 1)
                    if not proj and 1 + KC <= t < 1 + KC + IC:
                        down_weights_lo(0, 0, t - 1 - KC)
                    if att and t + 1 < NT:
                        heads_lo(i, t + 1)
                    if att and proj and t >= 6:
                        v_lo_part(p, t - 6, t - 2)
                    if not proj and t >= 2:
                        third_norm(t - 2)
                    if not proj and t >= 3:
                        transposed_lo(NT, t - 3, 4 + (t - 3) % 2)
                if att:
                    add_output(i, NT - 1)
                if split:
                    for c in range(2):
                        dve.wait_ge(wkv_hi_done, ev(i + 2, 2, c))
                        wkv_lo_chunk(c)

            key_norm(0, 0)
            key_norm(0, 1)
            key_lo(0, 0)
            key_lo(0, 1)
            iteration(-1, False, True, True)
            dve.wait_ge(x1_moved, 64)
            with dve.Fori(0, G - 2) as i:
                iteration(i, True, True, True)
            iteration(G - 2, True, True, False)
            iteration(G - 1, True, False, False)
            third_stats(NT - 1)
            third_norm(NT - 2)
            transposed_lo(NT, NT - 3, 4 + (NT - 3) % 2)
            third_norm(NT - 1)
            transposed_lo(NT, NT - 2, 4 + (NT - 2) % 2)
            transposed_lo(NT, NT - 1, 4 + (NT - 1) % 2)

            def shared_z(u):
                dve.wait_ge(silu_done, u + 1)
                if u >= 2:
                    dve.wait_ge(z_split, u - 1)
                dve.scalar_tensor_tensor(z32[:, u % 2, :], ps[:, 2 * (u % 3) + 1, :], 1.0 / WS, silu[:, u % 2, :],
                                         ALU.mult, ALU.mult).then_inc(z32_done, 1)

            dve.wait_ge(sig_exp, 1)
            then(dve.tensor_scalar(score[:, :, :], score[:, :, :], 1.0, None, ALU.add))
            then(dve.reciprocal(score[:, :, :], score[:, :, :]))
            then(dve.tensor_tensor(score[:, :, :], score[:, :, :],
                                   bias_sb[:, :].unsqueeze(1).to_broadcast([P, NT, E]), ALU.add))
            for t in range(NT):
                last = dve.max(top8[:, t, :], score[:, t, :])
            then(last)
            then(dve.tensor_reduce(wsum[:, :], top8[:, :, 0:TOPK], AX.X, ALU.add))
            then(dve.memset(top8[:, :, TOPK:8], -NEG))
            for t in range(NT):
                last = dve.match_replace(left[:, t, :], top8[:, t, :], score[:, t, :], NEG)
            then(last)
            dve.tensor_tensor(sel[:, :, :], left[:, :, :], score[:, :, :], ALU.not_equal).then_inc(sel_done, 1)
            dve.tensor_scalar(wsum[:, :], wsum[:, :], 1e-20, WS, ALU.add, ALU.mult).then_inc(sel_done, 1)
            shared_z(0)

            dve.wait_ge(rank_ps, 1)
            rank = ps[:, 6, 0:NT * E].rearrange("p (t e) -> p t e", e=E)
            total = ps[:, 6, NT * E:(NT + 1) * E]
            then(dve.tensor_tensor(need[:, :, :], total.unsqueeze(2).to_broadcast([P, E, NJT]),
                                   tile_steps[:, :].unsqueeze(1).to_broadcast([P, E, NJT]), ALU.is_gt))
            then(dve.tensor_reduce(tiles[:, :], need[:, :, :], AX.X, ALU.add))
            then(dve.tensor_tensor(before[:, :, :], before[:, :, :],
                                   tiles[:, :].unsqueeze(1).to_broadcast([P, E, E]), ALU.mult))
            then(dve.tensor_reduce(first_tile[:, :], before[:, :, :], AX.X, ALU.add))
            then(dve.tensor_tensor(past_tile[:, :], first_tile[:, :], tiles[:, :], ALU.add))
            shared_z(1)
            then(dve.tensor_scalar(first_tile[:, :], first_tile[:, :], float(TS), 1.0, ALU.mult, ALU.add))
            then(dve.tensor_tensor(key[:, :, :], rank, first_tile[:, :].unsqueeze(1).to_broadcast([P, NT, E]), ALU.add))
            then(dve.tensor_tensor(key[:, :, :], key[:, :, :], sel[:, :, :], ALU.mult))
            for t in range(NT):
                last = dve.max(key8[:, t, :], key[:, t, :])
            then(last)
            then(dve.tensor_scalar(slot[:, :].rearrange("p (t k) -> p t k", k=TOPK), key8[:, :, 0:TOPK], -1.0, None,
                                   ALU.add))
            hi_cmp, lo_cmp = steps_cmp[:, :, :], steps_cmp[:, :, 0:HI8 - 1]
            then(dve.tensor_tensor(hi_cmp, slot[:, :].unsqueeze(2).to_broadcast([P, NTK, HI8]),
                                   hi_steps[:, :].unsqueeze(1).to_broadcast([P, NTK, HI8]), ALU.is_ge))
            then(dve.tensor_reduce(slot_hi[:, :], hi_cmp, AX.X, ALU.add))
            then(dve.scalar_tensor_tensor(slot_rest[:, :], slot_hi[:, :], -float(HI8 * SW), slot[:, :],
                                          ALU.mult, ALU.add))
            then(dve.tensor_tensor(lo_cmp, slot_rest[:, :].unsqueeze(2).to_broadcast([P, NTK, HI8 - 1]),
                                   lo_steps[:, :].unsqueeze(1).to_broadcast([P, NTK, HI8 - 1]), ALU.is_ge))
            then(dve.tensor_reduce(slot_lo[:, :], lo_cmp, AX.X, ALU.add))
            dve.scalar_tensor_tensor(slot_a[:, :], slot_hi[:, :], float(HI8), slot_lo[:, :], ALU.mult, ALU.add)
            then(dve.scalar_tensor_tensor(slot_b[:, :], slot_lo[:, :], -float(SW), slot_rest[:, :], ALU.mult, ALU.add))
            shared_z(2)
            dve.tensor_tensor(on_a, slot_a[:, :].unsqueeze(2).to_broadcast([P, NTK, NS]),
                              count16[:, 0:NS].unsqueeze(1).to_broadcast([P, NTK, NS]), ALU.is_equal).then_inc(onehots, 1)
            shared_z(3)
            dve.tensor_tensor(on_b, slot_b[:, :].unsqueeze(2).to_broadcast([P, NTK, SW]),
                              count16[:, 0:SW].unsqueeze(1).to_broadcast([P, NTK, SW]), ALU.is_equal).then_inc(onehots, 1)
            dve.wait_ge(sel_done, 2)
            dve.tensor_tensor(cw[:, :, :], sel[:, :, :], score[:, :, :], ALU.mult)
            then(dve.reciprocal(wsum[:, :], wsum[:, :]))
            dve.tensor_tensor(cw[:, :, :], cw[:, :, :], wsum[:, :].unsqueeze(2).to_broadcast([P, NT, E]),
                              ALU.mult).then_inc(cw_done, 1)
            then(dve.tensor_tensor(tile_cmp[:, :, :], past_tile[:, :].unsqueeze(1).to_broadcast([P, TILES, E]),
                                   count_up[:, 0:TILES].unsqueeze(2).to_broadcast([P, TILES, E]), ALU.is_le))
            then(dve.tensor_reduce(eid[:, :], tile_cmp[:, :, :], AX.X, ALU.add))
            then(dve.tensor_scalar(eid[:, :], eid[:, :], float(E - 1), None, ALU.min))
            dve.tensor_copy(eid_int[:, :], eid[:, :]).then_inc(eid_done, 1)
            def shared_add(t):
                dve.wait_ge(d_ps, t + 1)
                dve.scalar_tensor_tensor(x_res[:, t, :], ps[:, t % 7, :], 1.0 / WS, x_res[:, t, :],
                                         ALU.mult, ALU.add).then_inc(d_added, 1)

            shared_add(0)
            dve.wait_ge(slot_ps, 1)
            then(dve.scalar_tensor_tensor(dump[0:SW, :], ps[0:SW, 7, 0:NS], 0.0, dump_no[0:SW, :],
                                          ALU.is_equal, ALU.mult))
            then(dve.scalar_tensor_tensor(row_f[0:SW, :], ps[0:SW, 7, 0:NS], float(T), dump[0:SW, :],
                                          ALU.add, ALU.add))
            dve.tensor_copy(to_row[0:SW, :], row_f[0:SW, :])
            dve.tensor_scalar(from_row[0:SW, :], row_f[0:SW, :], float(T - 1), None, ALU.min).then_inc(rows_done, 1)
            for t in range(1, NT):
                shared_add(t)
            for c in range(KC):
                expert_weights_lo(1, 1, c)
            then(dve.tensor_tensor(is_eid[:, :, :], eid[:, :].unsqueeze(2).to_broadcast([P, TILES, E]),
                                   count_up[:, 0:E].unsqueeze(1).to_broadcast([P, TILES, E]), ALU.is_equal))

            def slots_lo(r, par):
                for j in range(2):
                    dve.wait_ge(tT_hi_done, 2 * (r - 1) + j + 1)
                    dve.tensor_tensor(tT_lo[par][:, 2 * j:2 * j + 2, :],
                                      ps[:, 4 + j, 0:2 * TS].rearrange("p (k s) -> p k s", k=2),
                                      tT_hi[par][:, 2 * j:2 * j + 2, :], ALU.subtract).then_inc(tT_split, 1)

            def gated_up(r, n, c):
                dve.wait_ge(tsilu_done, 2 * (r - 1) + c + 1)
                if n >= 2:
                    dve.wait_ge(tz_split, 2 * (r - 2) + c + 1)
                dve.scalar_tensor_tensor(tz32[:, c, :], ps[:, c, 256:256 + TS], 1.0 / WS, tsilu[:, c, :],
                                         ALU.mult, ALU.mult).then_inc(tz32_done, 1)

            def slot_weights(r, par):
                dve.wait_ge(gathered[par], slots_read(r, par))
                dve.tensor_tensor(cw_cmp[0:SW, par, :, :], h_slot[par][0:SW, :, D:HROW],
                                  is_eid[0:SW, bass.ds(r - 1, 1), :].to_broadcast([SW, 2, E]),
                                  ALU.mult).then_inc(cw_cmp_done, 1)

            def slot_weights_sum(r, par, n):
                dve.wait_ge(cw_cmp_done, r)
                if n >= 3:
                    dve.wait_ge(y_done, 2 * (r - 2))
                dve.tensor_reduce(cw_slot[0:SW, par, :], cw_cmp[0:SW, par, :, :], AX.X, ALU.add).then_inc(cw_slot_done, 1)

            def step(r, par, n):
                more = n < TILES
                if more:
                    slots_lo(r + 1, 1 - par)
                    slot_weights(r + 1, 1 - par)
                    expert_weights_lo(r + 1, 1 - par, 0)
                    expert_weights_lo(r + 1, 1 - par, 1)
                gated_up(r, n, 0)
                if more:
                    expert_weights_lo(r + 1, 1 - par, 2)
                    expert_weights_lo(r + 1, 1 - par, 3)
                gated_up(r, n, 1)
                for c in range(IC):
                    down_weights_lo(r, par, c)
                if more:
                    slot_weights_sum(r + 1, 1 - par, n + 1)

            slots_lo(1, 1)
            slot_weights(1, 1)
            slot_weights_sum(1, 1, 1)
            rounds(dve, step)

        @block.tensor
        def _(pe):
            def product(dst, terms, chunks):
                n = len(terms) * len(chunks)
                m = 0
                for c in chunks:
                    for lhsT, rhs in terms:
                        last = pe.matmul(dst, lhsT(c), rhs(c), start=(m == 0), stop=(m == n - 1))
                        m += 1
                return last

            def parts(lhs_hi, lhs_lo, rhs_hi, rhs_lo):
                return [(lhs_hi, rhs_hi), (lhs_hi, rhs_lo), (lhs_lo, rhs_hi)]

            pe.wait_ge(consts, 14)
            pe.wait_ge(stats1, 1)
            pe.matmul(ps[:, 7, 0:2 * B], swap[:, :], mv[:, :, :].rearrange("p n s -> p (n s)"),
                      start=True, stop=True).then_inc(swapped, 1)
            pe.wait_ge(h1_done, B)
            pe.wait_ge(var_ready, 1)
            for t in range(8):
                if t >= 4:
                    pe.wait_ge(qT1_done, t - 3)
                for j in range(4):
                    l0 = LG * (4 * t + j)
                    last = pe.transpose(ps[:, 4 + t % 4, j * P:(j + 1) * P],
                                        hq[:, l0:l0 + LG, :].rearrange("p l n -> p (l n)"), ident[:, :])
                last.then_inc(qT1_ps, 1)
            for jh in range(2):
                for half in range(2):
                    rows = slice(half * S, half * S + S)
                    for j in range(16):
                        for k in range(4):
                            l0 = LG * (16 * jh + j) + 2 * k
                            q2 = hq[rows, l0:l0 + 2, :].rearrange("p l n -> p (l n)")
                            last = pe.matmul(ps[32 * k:32 * k + 32, 2 * jh + half, 32 * j:32 * j + 32], q2, q2,
                                             start=True, stop=True)
                    last.then_inc(gram, 1)
            pe.wait_ge(qT1_done, 8)
            for jh in range(2):
                pe.wait_ge(diag_done, 8 * jh + 8)
                if jh == 1:
                    pe.wait_ge(s1_shift, 4)
                for u in range(4):
                    for half in range(2):
                        for j in range(4 * u, 4 * u + 4):
                            last = pe.matmul(ps[half * S:half * S + S, 4 * (1 - jh) + u, (j % 4) * P:(j % 4 + 1) * P],
                                             qT1[:, 16 * jh + j, half * S:half * S + S],
                                             p1_diag[2 * jh + half][:, j, :], start=True, stop=True)
                    last.then_inc(msg, 1)

            def transpose_rows(t):
                pe.wait_ge(h2_done, 2 * t + 2)
                if t >= 4:
                    pe.wait_ge(hT_split, t - 3)
                cols = ps[:, t % 4, :].rearrange("p (h k b c) -> p k b h c", h=2, k=2, b=2)
                for b in range(2):
                    for k in range(2):
                        last = pe.transpose(cols[:, k, b, :, :], h2[:, 2 * t + b, k * P:(k + 1) * P], ident[:, :])
                last.then_inc(hT_ps, 1)

            def transpose_tokens(t, bank):
                pe.wait_ge(h_done, t + 1)
                if t >= 2:
                    pe.wait_ge(hT_split, NT + t - 1)
                for c in range(KC):
                    last = pe.transpose(ps[:, bank, c * P:(c + 1) * P], h_tok[:, t, c * P:(c + 1) * P], ident[:, :])
                last.then_inc(hT_ps, 1)

            def scores(i, b):
                if b == 0:
                    pe.wait_ge(q_split, 8 * i + 8)
                    pe.wait_ge(k_split, 2 * i + 2)
                for t in range(2):
                    for m in range(2):
                        for r in range(2):
                            n = 2 * (2 * b + t) + r
                            col = ((t * 2 + m) * 2 + r) * S
                            last = product(
                                ps[:, b, col:col + S],
                                parts(lambda _: q_hi[:, m, n, :, :].rearrange("p h s -> p (h s)"),
                                      lambda _: q_lo[:, m, n, :, :].rearrange("p h s -> p (h s)"),
                                      lambda _: k_hi[:, n * S:(n + 1) * S],
                                      lambda _: k_lo[:, n * S:(n + 1) * S]), [0])
                last.then_inc(s_ps, 1)

            def project_q(p, u):
                j, th = u // 2, u % 2
                if u == 0:
                    pe.wait_ge(wq_split, p * KC + KC)
                if u >= 2:
                    pe.wait_ge(q_split, ev(p, 8, u - 2))
                cols = slice(th * BANK, (th + 1) * BANK)
                heads = slice(j * HD, (j + 1) * HD)
                product(ps[:, 4 + u % 2, :],
                        parts(lambda c: wq_hi[:, c, heads], lambda c: wq_lo[:, c, heads],
                              lambda c: hT_hi[:, c, cols], lambda c: hT_lo[:, c, cols]),
                        range(KC)).then_inc(q_ps, 1)

            def project_k(p, th):
                if th == 0:
                    pe.wait_ge(wkv_split, p * 2 + 2)
                cols = slice(th * BANK, (th + 1) * BANK)
                product(ps[:, 4 + th, :],
                        parts(lambda c: wkv_hi[:, c, 0:HD], lambda c: wkv_lo[:, c, 0:HD],
                              lambda c: ctx_hi[:, c, cols], lambda c: ctx_lo[:, c, cols]),
                        range(KC)).then_inc(k_ps, 1)

            def project_v(p, th, bank):
                for t in range(4 * th, 4 * th + 4):
                    rows = slice(t * P, (t + 1) * P)
                    last = product(ps[:, bank, (t % 4) * HD:(t % 4 + 1) * HD],
                                   parts(lambda c: ctx_hi[:, c, rows], lambda c: ctx_lo[:, c, rows],
                                         lambda c: wkv_hi[:, c, HD:2 * HD], lambda c: wkv_lo[:, c, HD:2 * HD]),
                                   range(KC))
                last.then_inc(v_ps, 1)

            def sum_q_squares(p):
                pe.wait_ge(sq_split, 8 * p + 8)
                for t in range(NT):
                    for m in range(2):
                        for r in range(2):
                            col = (t * 2 + m) * 2 + r
                            for n, part in enumerate((sq_hi, sq_lo)):
                                last = pe.matmul(ps[:, 3, col:col + 1],
                                                 part[:, m, 2 * t + r, :, :].rearrange("p h s -> p (h s)"),
                                                 ones[:, 0:1], start=(n == 0), stop=(n == 1))
                last.then_inc(ssq_q_ps, 1)

            def sum_k_squares(p, th):
                pe.wait_ge(ksq_split, ev(p, 2, th))
                pe.matmul(ps[:, 4 + th, :], ones[:, :], ksq_hi[:, th, :], start=True, stop=False)
                pe.matmul(ps[:, 4 + th, :], ones[:, :], ksq_lo[:, th, :], start=False, stop=True).then_inc(ssq_k_ps, 1)

            def transpose_probs(i, t):
                b = t // 2
                if t % 2 == 0:
                    pe.wait_ge(prob_done, ev(i, 4, b))
                if t >= 2:
                    pe.wait_ge(pT_split, ev(i, NT, t - 2))
                for m in range(2):
                    col = ((t % 2) * 2 + m) * P
                    last = pe.transpose(ps[:, 6 + t % 2, m * P:(m + 1) * P], prob[:, b, col:col + P], ident[:, :])
                last.then_inc(pT_ps, 1)

            def heads_out(i, t):
                pe.wait_ge(pT_split, ev(i, NT, t))
                if t == 0:
                    pe.wait_ge(scaled, 4 * i + 4)
                else:
                    pe.wait_ge(o_split, ev(i, NT, t - 1))
                for n, (v, pt) in enumerate(((v_hi, pT_hi), (v_hi, pT_lo), (v_lo, pT_hi))):
                    for r in range(2):
                        rows = slice(r * S, (r + 1) * S)
                        last = pe.matmul(ps[:, r, 0:256], v[rows, t, :], pt[rows, t, :],
                                         start=(n == 0), stop=(n == 2))
                last.then_inc(pv_ps, 1)

            def output(i, t, hi, lo):
                pe.wait_ge(o_split, ev(i, NT, t))
                if t == 0:
                    pe.wait_ge(wo_split, HG * i + HG)
                if t >= 2:
                    pe.wait_ge(o_added, ev(i, NT, t - 2))
                product(ps[:, 2 + t % 2, :],
                        parts(lambda h: o_hi[:, h, t, :, :].rearrange("p b s -> p (b s)"),
                              lambda h: o_lo[:, h, t, :, :].rearrange("p b s -> p (b s)"),
                              lambda h: hi[:, h, :], lambda h: lo[:, h, :]),
                        range(HG)).then_inc(o_ps, 1)

            def iteration(i, att, proj, first=False):
                p = i + 1
                if att:
                    for b in range(4):
                        if not first and b >= 2:
                            pe.wait_ge(o_added, i * NT + (b - 3))
                        if first and b == 3:
                            pe.wait_ge(ln_q, 1)
                        scores(i, b)
                if proj:
                    for u in range(8):
                        if u < 2:
                            if att:
                                pe.wait_ge(v_split, ev(i, 2, u))
                            else:
                                pe.wait_ge(hT_split, 4 * u + 4)
                                pe.wait_ge(ln_k, u + 1)
                        project_q(p, u)
                    if att:
                        for th in range(2):
                            pe.wait_ge(q_split, ev(p, 8, 6 + th))
                            project_k(p, th)
                    else:
                        pe.wait_ge(v_split, 2)
                        sum_q_squares(p)
                if att:
                    transpose_probs(i, 0)
                    transpose_probs(i, 1)
                    if proj:
                        sum_k_squares(p, 0)
                    heads_out(i, 0)
                    if proj:
                        sum_q_squares(p)
                    for t in range(NT):
                        if t + 2 < NT:
                            transpose_probs(i, t + 2)
                        if t + 1 < NT:
                            heads_out(i, t + 1)
                        if proj and t >= 6:
                            pe.wait_ge(ln_k, ev(p, 2, t - 6))
                            project_v(p, t - 6, t - 2)
                        if not proj and t >= 3:
                            transpose_tokens(t - 3, 4 + (t - 3) % 2)
                        if proj and t == 1:
                            pe.wait_ge(ln_q, p + 1)
                        output(i, t, *((wo_hi, wo_lo) if proj else (wq_hi, wq_lo)))
                        if proj and t == 0:
                            sum_k_squares(p, 1)

            pe.wait_ge(ctx_split, KC)
            for th in range(2):
                pe.wait_ge(x1_done, th + 1)
                project_k(0, th)
            pe.wait_ge(stats1, 2)
            pe.matmul(ps[:, 0, 0:2 * B], swap[:, :], mv[:, :, :].rearrange("p n s -> p (n s)"),
                      start=True, stop=True).then_inc(swapped, 1)
            for th in range(2):
                project_v(0, th, 6 + th)
            pe.wait_ge(var_ready, 2)
            transpose_rows(0)
            transpose_rows(1)
            sum_k_squares(0, 0)
            sum_k_squares(0, 1)
            for t in range(2, NT):
                transpose_rows(t)
            iteration(-1, False, True)
            iteration(0, True, True, first=True)
            with pe.Fori(1, G - 1) as i:
                iteration(i, True, True)
            iteration(G - 1, True, False)
            transpose_tokens(NT - 3, 4 + (NT - 3) % 2)

            def shared_unit(u):
                if u == 0:
                    pe.wait_ge(wgu_split, KC)
                    pe.wait_ge(hT_split, NT + 4)
                if u == 2:
                    pe.wait_ge(hT_split, 2 * NT)
                if u == 1:
                    pe.wait_ge(o_added, NT * G)
                if u == 3:
                    pe.wait_ge(z32_done, 1)
                c, th = u % 2, u // 2
                cols = slice(th * BANK, (th + 1) * BANK)
                for gu in range(2):
                    w = slice(gu * I + c * P, gu * I + (c + 1) * P)
                    last = product(ps[:, 2 * (u % 3) + gu, :],
                                   parts(lambda k: wgu_hi[0][:, k, w], lambda k: wgu_lo[0][:, k, w],
                                         lambda k: hT_hi[:, k, cols], lambda k: hT_lo[:, k, cols]), range(KC))
                last.then_inc(gu_ps, 1)

            shared_unit(0)
            transpose_tokens(NT - 2, 4 + (NT - 2) % 2)
            transpose_tokens(NT - 1, 4 + (NT - 1) % 2)

            pe.wait_ge(gate_split, 1)
            pe.wait_ge(hT_split, 2 * NT)
            for t in range(NT):
                rows = slice(t * P, (t + 1) * P)
                last = product(ps[:, 7, t * E:(t + 1) * E],
                               parts(lambda c: hT_hi[:, c, rows], lambda c: hT_lo[:, c, rows],
                                     lambda c: gate_hi[:, c, :], lambda c: gate_lo[:, c, :]), range(KC))
            last.then_inc(logits, 1)

            def shared_down(t):
                if t % 4 == 0:
                    pe.wait_ge(z_split, 2 + t // 2)
                if t == 0:
                    pe.wait_ge(wd_split, IC)
                    pe.wait_ge(z32_done, 4)
                if t == 6:
                    pe.wait_ge(onehots, 1)
                if t == 7:
                    pe.wait_ge(d_added, 1)
                rows = slice(t * P, (t + 1) * P)
                product(ps[:, t % 7, :],
                        parts(lambda c: z_hi[:, c, rows], lambda c: z_lo[:, c, rows],
                              lambda c: wd_hi[0][:, c, :], lambda c: wd_lo[0][:, c, :]), range(IC)).then_inc(d_ps, 1)

            shared_unit(1)
            pe.wait_ge(sel_done, 1)
            for t in range(NT + 1):
                for k in range(min(t + 1, NT)):
                    last = pe.matmul(ps[:, 6, t * E:(t + 1) * E], below[:, :] if k == t else ones[:, :], sel[:, k, :],
                                     start=(k == 0), stop=(k == min(t, NT - 1)))
            last.then_inc(rank_ps, 1)
            for u in range(2, 4):
                shared_unit(u)
            for t in range(7):
                shared_down(t)
            pe.wait_ge(onehots, 2)
            pe.wait_ge(tokens_set, NT)
            for k in range(NTK):
                last = pe.matmul(ps[0:SW, 7, 0:NS], on_b[:, k, :], on_tok[:, k, :], start=(k == 0), stop=(k == NTK - 1))
            last.then_inc(slot_ps, 1)
            shared_down(7)

            def transpose_slots(r, par, n):
                pe.wait_ge(gathered[par], slots_read(r, par))
                if n >= 2:
                    pe.wait_ge(tT_split, 2 * (r - 1))
                for j in range(2):
                    for k in range(2):
                        for h in range(2):
                            c = 2 * j + k
                            col = k * TS + h * SW
                            last = pe.transpose(ps[:, 4 + j, col:col + SW], h_slot[par][0:SW, h, c * P:(c + 1) * P],
                                                ident[0:SW, 0:SW])
                    last.then_inc(tT_ps, 1)

            def gate_up(r, par, n):
                pe.wait_ge(tT_split, 2 * r)
                pe.wait_ge(wgu_split, KC * r + KC)
                for c in range(IC):
                    if n >= 2:
                        pe.wait_ge(tz32_done, 2 * (r - 2) + c + 1)
                    for gu in range(2):
                        w = slice(gu * I + c * P, gu * I + (c + 1) * P)
                        last = product(ps[:, c, 256 * gu:256 * gu + TS],
                                       parts(lambda k: wgu_hi[par][:, k, w], lambda k: wgu_lo[par][:, k, w],
                                             lambda k: tT_hi[par][:, k, :], lambda k: tT_lo[par][:, k, :]), range(KC))
                    last.then_inc(tgu_ps, 1)

            def down(r, par, n):
                pe.wait_ge(wd_split, IC * r + IC)
                pe.wait_ge(tz_split, 2 * r)
                for h in range(2):
                    if n >= 2:
                        pe.wait_ge(y_done, 2 * (r - 2) + h + 1)
                    rows = slice(h * SW, (h + 1) * SW)
                    product(ps[0:SW, 6 + h, :],
                            parts(lambda c: tz_hi[par][:, c, rows], lambda c: tz_lo[par][:, c, rows],
                                  lambda c: wd_hi[par][:, c, :], lambda c: wd_lo[par][:, c, :]),
                            range(IC)).then_inc(td_ps, 1)

            def step(r, par, n):
                if n < TILES:
                    transpose_slots(r + 1, 1 - par, n + 1)
                if n == 1:
                    pe.wait_ge(d_added, NT)
                gate_up(r, par, n)
                if n >= 2:
                    down(r - 1, 1 - par, n - 1)

            pe.wait_ge(d_added, 6)
            transpose_slots(1, 1, 1)
            rounds(pe, step)
            down(TILES, TILES % 2, TILES)


def kernel(x, ctx_4096, mask_1x1xSxS2_ff0, L0_xattn_Wq, L0_xattn_Wk, L0_xattn_Wv, L0_xattn_Wo,
           L0_xattn_q_norm_w, L0_xattn_k_norm_w, L0_ffn_gate_w, L0_ffn_bias, L0_ffn_Wg, L0_ffn_Wu,
           L0_ffn_Wd, L0_ffn_Sg, L0_ffn_Su, L0_ffn_Sd):
    import numpy as np
    import concourse.bacc as bacc
    from concourse.bass_utils import run_bass_kernel_spmd

    def chunked(w):
        w = np.swapaxes(w, -1, -2)
        return np.swapaxes(w.reshape(*w.shape[:-2], w.shape[-2] // P, P, w.shape[-1]), -3, -2)

    a = [np.asarray(v) for v in (L0_xattn_Wq, L0_xattn_Wk, L0_xattn_Wv, L0_xattn_Wo, L0_ffn_Wg, L0_ffn_Wu,
                                 L0_ffn_Wd, L0_ffn_Sg, L0_ffn_Su, L0_ffn_Sd)]
    Wq, Wk, Wv, Wo, Wg, Wu, Wd, Sg, Su, Sd = a
    kv = np.concatenate([Wk.reshape(G, HD, D), Wv.reshape(G, HD, D)], axis=1)
    gu = np.concatenate([np.concatenate([Wg, Sg[None]]), np.concatenate([Wu, Su[None]])], axis=1)
    down = np.concatenate([Wd, Sd[None]])
    arrays = {
        "x_half": np.asarray(x).reshape(B, S, 2, HALF).transpose(2, 1, 0, 3).reshape(P, B * HALF),
        "ctx_t": np.asarray(ctx_4096).reshape(T, KC, P).transpose(2, 1, 0).reshape(P, KC * T),
        "mask": np.asarray(mask_1x1xSxS2_ff0).reshape(S, S),
        "wq": chunked(Wq.reshape(G, HG * HD, D)),
        "wkv": chunked(kv),
        "wo": Wo.reshape(D, G, HG, HD).transpose(1, 3, 2, 0),
        "qk_norm": np.stack([np.asarray(L0_xattn_q_norm_w), np.asarray(L0_xattn_k_norm_w)], axis=1),
        "gate_t": chunked(np.asarray(L0_ffn_gate_w)).reshape(P, KC * E),
        "bias": np.broadcast_to(np.asarray(L0_ffn_bias), (P, E)),
        "wgu": chunked(gu),
        "wd": chunked(down),
    }
    nc = bacc.Bacc("TRN2", target_bir_lowering=False, num_devices=1)
    arrays = {f"in_{k}": np.ascontiguousarray(v) for k, v in arrays.items()}
    args = [nc.dram_tensor(k, v.shape, F32, kind="ExternalInput").ap() for k, v in arrays.items()]
    h_rows = nc.dram_tensor("h_rows", (T, HROW), F32).ap()
    out = nc.dram_tensor("out_x", (T + TS, D), F32, kind="ExternalOutput").ap()
    decoder_kernel(nc, *args, h_rows, out)
    r = run_bass_kernel_spmd(nc, [arrays], core_ids=[0])
    return r.results[0]["out_x"][0:T].reshape(B, S, D)
```

```python
from contextlib import ExitStack

import concourse.bass as bass
from concourse import mybir

F32 = mybir.dt.float32
F16 = mybir.dt.float16
BF16 = mybir.dt.bfloat16
I32 = mybir.dt.int32
ALU = mybir.AluOpType
ACT = mybir.ActivationFunctionType
AX = mybir.AxisListType

P = 128
B, S, D = 16, 64, 512
T = B * S
NT = T // P
KC = D // P
H, G, HD = 32, 8, 128
HG = H // G
E, I = 16, 256
TOPK = 4
SHARED = E
IC = I // P
SW = 128
TS = 2 * SW
TILES = (T * TOPK + E * (TS - 1)) // TS
NS = 2 * TILES
NTK = NT * TOPK
NJT = -(-T // TS)
HI8 = 8
HROW = D + E
EPS = 1e-5
WS = 64.0
NEG = -1e30

LATE = 2
HALF = D // 2
LG = 8
NJ = HALF // LG
BANK = 512
ACT_ROWS = range(1, 12, 2)
DVE_ROWS = [n for n in range(B) if n not in ACT_ROWS]


def rows_to(rows, n):
    return sum(m <= n for m in rows)


def ev(i, per, j):
    return i * per + (j + 1)


def decoder_kernel(nc, x_half, ctx_t, mask, wq, wkv, wo, qk_norm, gate_t, bias, wgu, wd, h_rows, out):
    with ExitStack() as ctx:
        def sb(name, shape, dt=F32):
            return ctx.enter_context(nc.sbuf_tensor(name, shape, dt))

        def sem(name):
            return ctx.enter_context(nc.semaphore(name))

        ps = ctx.enter_context(nc.psum_tensor("ps", [P, 8, BANK], F32))

        ident = sb("ident", [P, P])
        swap = sb("swap", [P, P])
        blockmask = sb("blockmask", [P, 32])
        ident16 = sb("ident16", [P, P], BF16)
        blockmask16 = sb("blockmask16", [P, 32], BF16)
        ones = sb("ones", [P, P], F16)
        eps_ln = sb("eps_ln", [P, 1])
        eps_q = sb("eps_q", [P, 1])
        mask_sb = sb("mask_sb", [P, S])
        norm_sb = sb("norm_sb", [P, 2])
        wqk = sb("wqk", [P, 1])
        gate_st = sb("gate_st", [P, KC, E])
        gate_hi = sb("gate_hi", [P, KC, E], F16)
        gate_lo = sb("gate_lo", [P, KC, E], F16)
        bias_sb = sb("bias_sb", [P, E])
        bnst = sb("bnst", [P, B, 2, 6])
        mv = sb("mv", [P, B, 2])
        msum = sb("msum", [P, B, 2])
        mtmp = sb("mtmp", [P, B])
        mean = sb("mean", [P, B])
        lnvar = sb("lnvar", [P, B])
        rstd = sb("rstd", [P, B])
        shift_ln = sb("shift_ln", [P, B])
        smx = sb("smx", [P, 4, 16])
        ssum = sb("ssum", [P, 4, 16])
        sinv = sb("sinv", [P, 4, 16])

        x_res = sb("x_res", [P, NT, D])
        ctx_hi = sb("ctx_hi", [P, KC, T], F16)
        ctx_lo = sb("ctx_lo", [P, KC, T], F16)
        hT_hi = sb("hT_hi", [P, KC, T], F16)
        hT_lo = sb("hT_lo", [P, KC, T], F16)

        reg_x = sb("reg_x", [P, 4096])
        reg_h = sb("reg_h", [P, 4096])
        reg_a = sb("reg_a", [P, 4096])
        reg_b = sb("reg_b", [P, 4096])
        reg_c = sb("reg_c", [P, 4096])
        xh = reg_x[:, :].rearrange("p (n l) -> p n l", n=B)
        hq = reg_h[:, :].rearrange("p (l n) -> p l n", n=B)
        qT1 = reg_a[:, :].rearrange("p (j c) -> p j c", c=P)
        e1 = reg_b[:, 0:2048].rearrange("p (b c) -> p b c", c=BANK)
        p1T = reg_b[:, 2048:4096].rearrange("p (b c) -> p b c", c=BANK)
        ctx_st = reg_c[:, :].rearrange("p (k t) -> p k t", k=KC)
        p1_diag = [w.rearrange("p (j c) -> p j c", c=P) for w in (
            x_res[:, 0:4, :].rearrange("p t d -> p (t d)"), x_res[:, 4:8, :].rearrange("p t d -> p (t d)"),
            hT_hi[:, :, :].rearrange("p k t -> p (k t)").bitcast(F32),
            hT_lo[:, :, :].rearrange("p k t -> p (k t)").bitcast(F32))]
        h2 = reg_h[:, :].rearrange("p (n l) -> p n l", n=B)
        h_tok = reg_h[:, :].rearrange("p (t d) -> p t d", t=NT)

        def halves(region, n=2048):
            return region[:, 0:n].bitcast(F16), region[:, n:2 * n].bitcast(F16)

        q_hi, q_lo = (r.rearrange("p (m b h s) -> p m b h s", m=2, b=B, h=2) for r in halves(reg_a))
        sq_hi, sq_lo = (r.rearrange("p (m b h s) -> p m b h s", m=2, b=B, h=2) for r in halves(reg_c))
        o_hi, o_lo = (r.rearrange("p (h t b s) -> p h t b s", h=HG, t=NT, b=2) for r in halves(reg_b))
        prob = reg_x[:, 0:2048].rearrange("p (b c) -> p b c", c=BANK)
        pT_hi = reg_x[:, 2048:3072].bitcast(F16).rearrange("p (t c) -> p t c", t=NT)
        pT_lo = reg_x[:, 3072:4096].bitcast(F16).rearrange("p (t c) -> p t c", t=NT)

        wq_st = sb("wq_st", [P, KC, BANK])
        wq_hi = sb("wq_hi", [P, KC, BANK], F16)
        wq_lo = sb("wq_lo", [P, KC, BANK], F16)
        wkv_st = sb("wkv_st", [P, KC, 2 * HD])
        wkv_hi = sb("wkv_hi", [P, KC, 2 * HD], F16)
        wkv_lo = sb("wkv_lo", [P, KC, 2 * HD], F16)
        wo_st = sb("wo_st", [P, HG, D])
        wo_hi = sb("wo_hi", [P, HG, D], F16)
        wo_lo = sb("wo_lo", [P, HG, D], F16)
        sq32 = sb("sq32", [P, 2, BANK])
        k32 = sb("k32", [P, 2, BANK])
        ksq32 = sb("ksq32", [P, 2, BANK])
        ksq_hi = sb("ksq_hi", [P, 2, BANK], F16)
        ksq_lo = sb("ksq_lo", [P, 2, BANK], F16)
        rk = sb("rk", [P, 2, BANK])
        k_hi = sb("k_hi", [P, T], F16)
        k_lo = sb("k_lo", [P, T], F16)
        v_hi = sb("v_hi", [P, NT, HD], F16)
        v_lo = sb("v_lo", [P, NT, HD], F16)
        rq = sb("rq", [P, 32])
        rowmax = sb("rowmax", [P, 4, 8])
        rowsum = sb("rowsum", [P, 4, 8])
        rowinv = sb("rowinv", [P, 4, 8])

        def flat(buf):
            return buf[:, :, :].rearrange("p k n -> p (k n)")

        wgu_st = [reg[:, 0:2048].rearrange("p (k n) -> p k n", k=KC) for reg in (reg_c, reg_x)]
        wd_st = [reg[:, 2048:3072].rearrange("p (k n) -> p k n", k=IC) for reg in (reg_c, reg_x)]
        wgu_hi, wgu_lo = (wo_hi, wq_hi), (wo_lo, wq_lo)
        wd_hi = [w.rearrange("p (k n) -> p k n", k=IC) for w in (flat(wkv_hi), reg_x[:, 3072:3584].bitcast(F16))]
        wd_lo = [w.rearrange("p (k n) -> p k n", k=IC) for w in (flat(wkv_lo), reg_x[:, 3584:4096].bitcast(F16))]
        z_hi = reg_a[:, 0:1024].bitcast(F16).rearrange("p (c t) -> p c t", c=IC)
        z_lo = reg_a[:, 1024:2048].bitcast(F16).rearrange("p (c t) -> p c t", c=IC)
        silu = reg_a[:, 2048:3072].rearrange("p (u n) -> p u n", u=2)
        z32 = reg_a[:, 3072:4096].rearrange("p (u n) -> p u n", u=2)
        on_b = reg_b[:, 0:NTK * SW // 2].bitcast(F16).rearrange("p (c s) -> p c s", s=SW)
        on_a = reg_b[:, 2048:2048 + NTK * NS // 2].bitcast(F16).rearrange("p (c s) -> p c s", s=NS)
        on_tok = flat(wq_st)[:, 0:NTK * NS // 2].bitcast(F16).rearrange("p (c s) -> p c s", s=NS)
        def pair(region, col, n, dt=F32):
            words = n if dt == F32 else n // 2
            return [region[:, col + i * words:col + (i + 1) * words].bitcast(dt) if dt != F32 else
                    region[:, col + i * words:col + (i + 1) * words] for i in range(2)]

        tz_hi = [w.rearrange("p (c s) -> p c s", c=IC) for w in pair(reg_b, 0, IC * TS, F16)]
        tz_lo = [w.rearrange("p (c s) -> p c s", c=IC) for w in pair(reg_b, IC * TS, IC * TS, F16)]
        tsilu, tz32 = (w.rearrange("p (c s) -> p c s", c=IC) for w in pair(reg_a, 2048, IC * TS))
        h_slot = [w.rearrange("p (h d) -> p h d", h=2) for w in pair(reg_b, 2 * IC * TS, 2 * HROW)]
        tT_hi = [w.rearrange("p (k s) -> p k s", k=KC) for w in pair(flat(k32), 0, KC * TS, F16)]
        tT_lo = [w.rearrange("p (k s) -> p k s", k=KC) for w in pair(flat(ksq32), 0, KC * TS, F16)]
        down_bank = [2, 3, 4, 5, 0, 1, 6, 7]
        add_order = [2, 3, 4, 5, 0, 1, 6, 7]
        y = [w.rearrange("p (h d) -> p h d", h=2) for w in pair(reg_h, 0, 2 * D)]

        score = sb("score", [P, NT, E])
        left = sb("left", [P, NT, E])
        top8 = sb("top8", [P, NT, 8])
        sel = sb("sel", [P, NT, E], F16)
        wsum = sb("wsum", [P, NT])
        cw = sb("cw", [P, NT, E])
        below = sb("below", [P, P], F16)
        row_no = sb("row_no", [P, 1])
        count_up = sb("count_up", [P, P])
        count16 = sb("count16", [P, P], F16)
        tile_steps = sb("tile_steps", [P, NJT])
        hi_steps = sb("hi_steps", [P, HI8])
        lo_steps = sb("lo_steps", [P, HI8 - 1])
        tok_no = sb("tok_no", [P, NT])
        dump_no = sb("dump_no", [P, NS])
        before = sb("before", [P, E, E])
        tiles = sb("tiles", [P, E])
        first_tile = sb("first_tile", [P, E])
        past_tile = sb("past_tile", [P, E])
        eid = sb("eid", [P, TILES])
        eid_int = sb("eid_int", [P, TILES], I32)

        def carve(buf, *widths):
            ends = [sum(widths[:i]) for i in range(len(widths) + 1)]
            return [flat(buf)[:, i:j] for i, j in zip(ends, ends[1:])]

        tile_cmp, steps_cmp, key, key8 = carve(sq32, TILES * E, NTK * HI8, NT * E, NT * 8)
        tile_cmp = tile_cmp.rearrange("p (n e) -> p n e", e=E)
        steps_cmp = steps_cmp.rearrange("p (c j) -> p c j", j=HI8)
        key = key.rearrange("p (t e) -> p t e", e=E)
        key8 = key8.rearrange("p (t k) -> p t k", k=8)
        need, is_eid, slot, slot_hi, slot_lo, slot_rest, dump = carve(
            rk, E * NJT, TILES * E, NTK, NTK, NTK, NTK, NS)
        slot_a = sb("slot_a", [P, NTK], F16)
        slot_b = sb("slot_b", [P, NTK], F16)
        need = need.rearrange("p (e j) -> p e j", j=NJT)
        is_eid = is_eid.rearrange("p (n e) -> p n e", e=E)
        from_row = sb("from_row", [P, NS], I32)
        to_row = sb("to_row", [P, NS], I32)
        from_now = sb("from_now", [P, 2, 2], I32)
        to_now = sb("to_now", [P, 2, 2], I32)
        cw_cmp = sb("cw_cmp", [P, 2, 2, E])
        cw_slot = sb("cw_slot", [P, 2, 2])

        x_in = [sem(f"x_in{j}") for j in range(NT)]
        ctx_in, mask_in, small_in = sem("ctx_in"), sem("mask_in"), sem("small_in")
        wq_in, wkv_in, wo_in = sem("wq_in"), sem("wkv_in"), sem("wo_in")
        wgu_in = [sem(f"wgu_in{i}") for i in range(2)]
        wd_in = [sem(f"wd_in{i}") for i in range(2)]
        zeroed, consts, dve_consts = sem("zeroed"), sem("consts"), sem("dve_consts")
        chain = sem("chain")
        ctx_hi_done, ctx_split = sem("ctx_hi_done"), sem("ctx_split")
        stats1, swapped, var_ready, lnvar_ready, rstd_ready = (
            sem("stats1"), sem("swapped"), sem("var_ready"), sem("lnvar_ready"), sem("rstd_ready"))
        shift_ready, masks16 = sem("shift_ready"), sem("masks16")
        h1_dve, h1_act, x_plus_h = sem("h1_dve"), sem("h1_act"), sem("x_plus_h")
        weights_scaled = sem("weights_scaled")
        qT1_ps, qT1_done = sem("qT1_ps"), sem("qT1_done")
        gram, s1_shift, e1_done, p1_done = sem("gram"), sem("s1_shift"), sem("e1_done"), sem("p1_done")
        diag_zero, diag_done, h2_dve, h2_act = sem("diag_zero"), sem("diag_done"), sem("h2_dve"), sem("h2_act")
        msg, x1_done, x1_moved = sem("msg"), sem("x1_done"), sem("x1_moved")
        h_done, hT_ps, hT_hi_done, hT_split = sem("h_done"), sem("hT_ps"), sem("hT_hi_done"), sem("hT_split")
        wq_hi_done, wq_split = sem("wq_hi_done"), sem("wq_split")
        wkv_hi_done, wkv_split = sem("wkv_hi_done"), sem("wkv_split")
        wo_hi_done, wo_split = sem("wo_hi_done"), sem("wo_split")
        s_ps, q_ps, k_ps, v_ps = sem("s_ps"), sem("q_ps"), sem("k_ps"), sem("v_ps")
        ssq_q_ps, ssq_k_ps, pT_ps, pv_ps, o_ps = (
            sem("ssq_q_ps"), sem("ssq_k_ps"), sem("pT_ps"), sem("pv_ps"), sem("o_ps"))
        q_hi_done, sq32_done, sq_hi_done, sq_split, q_split = (
            sem("q_hi_done"), sem("sq32_done"), sem("sq_hi_done"), sem("sq_split"), sem("q_split"))
        scaled, masked, max_done, shifted, exp_done = (
            sem("scaled"), sem("masked"), sem("max_done"), sem("shifted"), sem("exp_done"))
        sum_done, inv_done, prob_done = sem("sum_done"), sem("inv_done"), sem("prob_done")
        pT_hi_done, pT_split, o_hi_done, o_split = (
            sem("pT_hi_done"), sem("pT_split"), sem("o_hi_done"), sem("o_split"))
        k32_done, ksq32_done, ksq_hi_done, ksq_split = (
            sem("k32_done"), sem("ksq32_done"), sem("ksq_hi_done"), sem("ksq_split"))
        v_hi_done, v_split, k_norm, k_hi_done, k_split = (
            sem("v_hi_done"), sem("v_split"), sem("k_norm"), sem("k_hi_done"), sem("k_split"))
        ln_q, rq_done, ln_k, rk_done, o_added = (
            sem("ln_q"), sem("rq_done"), sem("ln_k"), sem("rk_done"), sem("o_added"))
        gate_split, logits, sig_exp, cw_done = (
            sem("gate_split"), sem("logits"), sem("sig_exp"), sem("cw_done"))
        wgu_hi_done, wgu_split, wd_hi_done, wd_split = (
            sem("wgu_hi_done"), sem("wgu_split"), sem("wd_hi_done"), sem("wd_split"))
        gu_ps, silu_done, z32_done, z_hi_done, z_split = (
            sem("gu_ps"), sem("silu_done"), sem("z32_done"), sem("z_hi_done"), sem("z_split"))
        d_ps, d_added, stored = sem("d_ps"), sem("d_added"), sem("stored")
        numbers, h_stored = sem("numbers"), sem("h_stored")
        sel_done, rank_ps, eid_done, onehots, slot_ps, rows_done = (
            sem("sel_done"), sem("rank_ps"), sem("eid_done"), sem("onehots"), sem("slot_ps"), sem("rows_done"))
        now, scattered, tokens_set = sem("now"), sem("scattered"), sem("tokens_set")
        gathered = [sem(f"gathered{i}") for i in range(2)]

        tT_ps, tT_hi_done, tT_split, cw_slot_done = sem("tT_ps"), sem("tT_hi_done"), sem("tT_split"), sem("cw_slot_done")
        tgu_ps, tsilu_done, tz32_done, tz_hi_done, tz_split = (
            sem("tgu_ps"), sem("tsilu_done"), sem("tz32_done"), sem("tz_hi_done"), sem("tz_split"))
        cw_cmp_done = sem("cw_cmp_done")
        td_ps, y_done = sem("td_ps"), sem("y_done")

        def loaded(r, par):
            return r * 8 + (8 if par else 16)

        def slots_read(r, par):
            return r * 16 + (16 if par else 0)

        def rounds(eng, step):
            first, last = 4, 4 + (TILES - 3 - 4) // 2 * 2
            for r in range(1, first + 1):
                step(r, r % 2, r)
            with eng.Fori(first // 2, last // 2) as m:
                step(2 * m + 1, 1, first + 1)
                step(2 * m + 2, 0, first + 2)
            for r in range(last + 1, TILES + 1):
                step(r, r % 2, r)

        block = ctx.enter_context(nc.Block())

        @block.sync
        def _(sp):
            xh_d = x_half.rearrange("p (n l) -> p n l", n=B)
            for j in range(NT):
                sp.dma_start(xh[:, 2 * j:2 * j + 2, :], xh_d[:, 2 * j:2 * j + 2, :]).then_inc(x_in[j], 16)
            sp.dma_start(ctx_st, ctx_t.rearrange("p (k t) -> p k t", k=KC)).then_inc(ctx_in, 16)
            sp.dma_start(wq_st[:, :, :], wq[0]).then_inc(wq_in, 16)
            sp.dma_start(wkv_st[:, :, :], wkv[0]).then_inc(wkv_in, 16)
            sp.dma_start(wo_st[:, :, :], wo[0]).then_inc(wo_in, 16)
            x_pairs = xh.rearrange("p (t b) l -> p t b l", b=2)
            sp.wait_ge(x1_done, 8)
            for half in range(2):
                for b in range(2):
                    sp.dma_start(x_res[b * S:(b + 1) * S, :, half * HALF:(half + 1) * HALF],
                                 x_pairs[half * S:(half + 1) * S, :, b, :]).then_inc(x1_moved, 16)
            with sp.Fori(1, G) as g:
                sp.wait_ge(wq_split, g * KC)
                sp.dma_start(wq_st[:, :, :], wq[g]).then_inc(wq_in, 16)
                sp.wait_ge(wkv_split, g * 2)
                sp.dma_start(wkv_st[:, :, :], wkv[g]).then_inc(wkv_in, 16)
                sp.wait_ge(wo_split, g * HG)
                sp.dma_start(wo_st[:, :, :], wo[g]).then_inc(wo_in, 16)
            sp.wait_ge(ssq_q_ps, G)
            sp.dma_start(wgu_st[0], wgu[SHARED]).then_inc(wgu_in[0], 16)
            sp.dma_start(wd_st[0], wd[SHARED]).then_inc(wd_in[0], 16)
            rows = h_rows.rearrange("(t p) d -> p t d", p=P)
            sp.wait_ge(h_done, NT)
            sp.dma_start(rows[:, :, 0:D], h_tok).then_inc(h_stored, 16)
            for i in range(2):
                sp.dma_start(out[T + i * SW:T + (i + 1) * SW, :], h_tok[0:SW, i, :]).then_inc(h_stored, 16)
            sp.wait_ge(cw_done, 1)
            sp.dma_start(rows[:, :, D:HROW], cw[:, :, :]).then_inc(h_stored, 16)

            def load_expert(n, par):
                e = sp.value_load(eid_int[0:1, bass.ds(n, 1)], min_val=0, max_val=E - 1)
                return (wgu[bass.ds(e, 1), :, :, :].rearrange("o p k n -> p (o k) n"),
                        wd[bass.ds(e, 1), :, :, :].rearrange("o p k n -> p (o k) n"))

            def load_gate_up(r, par, src):
                sp.wait_ge(wgu_split, (r - 1) * KC)
                sp.dma_start(wgu_st[par], src).then_inc(wgu_in[par], 16)

            def load_down(r, par, src):
                sp.wait_ge(wd_split, (r - 1) * IC)
                sp.dma_start(wd_st[par], src).then_inc(wd_in[par], 16)

            def load_round(r, par):
                gu_src, d_src = load_expert(r - 1, par)
                load_gate_up(r, par, gu_src)
                load_down(r, par, d_src)

            sp.wait_ge(eid_done, 1)
            first = load_expert(0, 1)
            sp.dma_start(wgu_st[1], first[0]).then_inc(wgu_in[1], 16)
            second, third = load_expert(1, 0), load_expert(2, 1)
            sp.wait_ge(gathered[1], 32)
            load_gate_up(2, 0, second[0])
            sp.wait_ge(gathered[1], 64)
            sp.dma_start(wd_st[1], first[1]).then_inc(wd_in[1], 16)
            load_down(2, 0, second[1])
            load_gate_up(3, 1, third[0])
            fourth = load_expert(3, 0)
            for n, t in enumerate(add_order):
                if n == NT // 2:
                    sp.wait_ge(gathered[0], 64)
                    load_gate_up(4, 0, fourth[0])
                    load_down(3, 1, third[1])
                sp.wait_ge(d_added, n + 1)
                sp.dma_start(out[t * P:(t + 1) * P, :], x_res[:, t, :]).then_inc(stored, 16)
            load_down(4, 0, fourth[1])
            with sp.Fori(2, TILES // 2) as m:
                load_round(2 * m + 1, 1)
                load_round(2 * m + 2, 0)
            if TILES % 2:
                load_round(TILES, 1)
            sp.wait_ge(scattered, 2 * 16 * TILES)

        @block.gpsimd
        def _(pool):
            pool.memset(ident[:, :], 0.0).then_inc(zeroed, 1)
            pool.memset(swap[:, :], 0.0).then_inc(zeroed, 1)
            pool.memset(blockmask[:, :], 0.0).then_inc(zeroed, 1)
            pool.memset(ones[:, :], 1.0).then_inc(consts, 1)
            pool.memset(eps_ln[:, :], EPS).then_inc(consts, 1)
            pool.memset(eps_q[:, :], 4096.0 * HD * EPS).then_inc(consts, 1)
            pool.wait_ge(zeroed, 3)
            pool.affine_select(out=ident[:, :], in_=ident[:, :], compare_op=ALU.not_equal, fill=1.0,
                               base=0, pattern=[[-1, P]], channel_multiplier=1).then_inc(consts, 1)
            pool.affine_select(out=swap[:, 0:64], in_=swap[:, 0:64], compare_op=ALU.not_equal, fill=1.0,
                               base=-64, pattern=[[-1, 64]], channel_multiplier=1).then_inc(consts, 1)
            pool.affine_select(out=swap[:, 64:128], in_=swap[:, 64:128], compare_op=ALU.not_equal, fill=1.0,
                               base=0, pattern=[[-1, 64]], channel_multiplier=1).then_inc(consts, 1)
            for q in range(4):
                rows = slice(32 * q, 32 * q + 32)
                pool.wait_ge(consts, 6 + 2 * q)
                pool.affine_select(out=blockmask[rows, 0:16], in_=blockmask[rows, 0:16], compare_op=ALU.is_ge,
                                   fill=NEG, base=15, pattern=[[0, 16]], channel_multiplier=-1).then_inc(consts, 1)
                pool.wait_ge(consts, 7 + 2 * q)
                pool.affine_select(out=blockmask[rows, 16:32], in_=blockmask[rows, 16:32], compare_op=ALU.is_ge,
                                   fill=NEG, base=-16, pattern=[[0, 16]], channel_multiplier=1).then_inc(consts, 1)
            pool.wait_ge(consts, 14)

            iotas = [0]

            def iota(buf, pattern, base, per_row):
                if iotas[0]:
                    pool.wait_ge(numbers, iotas[0])
                iotas[0] += 1
                pool.iota(buf, pattern=pattern, base=base, channel_multiplier=per_row,
                          allow_small_or_imprecise_dtypes=True).then_inc(numbers, 1)

            iota(count_up[:, :], [[1, P]], 0, 0)
            iota(row_no[:, :], [[1, 1]], 0, 1)
            iota(tile_steps[:, :], [[TS, NJT]], 0, 0)
            iota(hi_steps[:, :], [[HI8 * SW, HI8]], HI8 * SW, 0)
            iota(lo_steps[:, :], [[SW, HI8 - 1]], SW, 0)
            iota(tok_no[:, :], [[P, NT]], -T, 1)
            iota(dump_no[:, :], [[0, TILES], [SW, 2]], 0, 1)
            pool.wait_ge(numbers, 7)
            for b in range(4):
                pool.memset(p1_diag[b], 0.0).then_inc(diag_zero, 1)
                pool.wait_ge(diag_zero, b + 1)
            pool.wait_ge(h1_dve, len(DVE_ROWS))
            pool.wait_ge(h1_act, len(ACT_ROWS))
            for j in range(4):
                n = slice(4 * j, 4 * j + 4)
                pool.tensor_tensor(xh[:, n, :], xh[:, n, :], hq[:, :, n].rearrange("p l n -> p n l"),
                                   ALU.add).then_inc(x_plus_h, 1)
            for c in range(KC):
                pool.wait_ge(ctx_hi_done, c + 1)
                pool.tensor_tensor(ctx_lo[:, c, :], ctx_st[:, c, :], ctx_hi[:, c, :],
                                   ALU.subtract).then_inc(ctx_split, 1)
            for c in range(2):
                pool.wait_ge(weights_scaled, c + 1)
                pool.tensor_tensor(wkv_lo[:, 2 * c:2 * c + 2, :], wkv_st[:, 2 * c:2 * c + 2, :],
                                   wkv_hi[:, 2 * c:2 * c + 2, :], ALU.subtract).then_inc(wkv_split, 1)
            for c in range(KC):
                pool.wait_ge(weights_scaled, 2 + c + 1)
                pool.tensor_tensor(wq_lo[:, c, :], wq_st[:, c, :], wq_hi[:, c, :], ALU.subtract).then_inc(wq_split, 1)
            pool.wait_ge(weights_scaled, 2 + KC + 1)
            pool.tensor_tensor(gate_lo[:, :, :], gate_st[:, :, :], gate_hi[:, :, :],
                               ALU.subtract).then_inc(gate_split, 1)

            def mask_add(i, b):
                pool.wait_ge(scaled, ev(i, 4, b))
                t = prob[:, b, :].rearrange("p (g k) -> p g k", k=S)
                pool.tensor_tensor(t, t, mask_sb[:, :].unsqueeze(1).to_broadcast([P, 8, S]),
                                   ALU.add).then_inc(masked, 1)

            def shift(i, b):
                pool.wait_ge(max_done, ev(i, 4, b))
                t = prob[:, b, :].rearrange("p (g k) -> p g k", k=S)
                pool.tensor_tensor(t, t, rowmax[:, b, :].unsqueeze(2).to_broadcast([P, 8, S]),
                                   ALU.subtract).then_inc(shifted, 1)

            def square_lo(p, u):
                j, th = u // 2, u % 2
                pool.wait_ge(sq_hi_done, ev(p, 8, u))
                w = sq_hi[:, j // 2, 8 * th:8 * th + 8, j % 2, :]
                pool.tensor_tensor(sq_lo[:, j // 2, 8 * th:8 * th + 8, j % 2, :],
                                   sq32[:, u % 2, :].rearrange("p (b s) -> p b s", s=S), w,
                                   ALU.subtract).then_inc(sq_split, 1)

            def k_square_lo(p, th):
                pool.wait_ge(ksq_hi_done, ev(p, 2, th))
                pool.tensor_tensor(ksq_lo[:, th, :], ksq32[:, th, :], ksq_hi[:, th, :],
                                   ALU.subtract).then_inc(ksq_split, 1)

            def iteration(i, att, proj):
                if att and proj:
                    for b in range(4):
                        mask_add(i, b)
                for k in range(8):
                    if att and not proj and k < 4:
                        mask_add(i, k)
                    if att and proj and k < 4:
                        shift(i, k)
                    if att and not proj and 1 <= k < 5:
                        shift(i, k - 1)
                    if proj:
                        square_lo(i + 1, k)
                if proj and att:
                    k_square_lo(i + 1, 0)
                    k_square_lo(i + 1, 1)

            k_square_lo(0, 0)
            k_square_lo(0, 1)
            iteration(-1, False, True)
            pool.wait_ge(mask_in, 32)
            with pool.Fori(0, G - 1) as i:
                iteration(i, True, True)
            iteration(G - 1, True, False)

            for u in range(4):
                pool.wait_ge(z_hi_done, u + 1)
                c, th = u % 2, u // 2
                cols = slice(th * BANK, th * BANK + BANK)
                pool.tensor_tensor(z_lo[:, c, cols], z32[:, u % 2, :], z_hi[:, c, cols],
                                   ALU.subtract).then_inc(z_split, 1)

            def gather_rows(par, rows):
                for h in range(2):
                    pool.indirect_dma_start(h_slot[par][0:SW, h, :], None, h_rows, bass.IndirectOffsetOnAxis(
                        ap=rows[0:SW, h:h + 1], axis=0)).then_inc(gathered[par], 16)

            def gather(r, par, copies):
                pool.tensor_copy(from_now[0:SW, par, :], from_row[0:SW, bass.ds((r - 1) * 2, 2)]).then_inc(now, 1)
                pool.wait_ge(now, copies)
                pool.nop(nofuse=True)
                gather_rows(par, from_now[:, par, :])

            def scatter(r, par, n, copies):
                pool.wait_ge(y_done, 2 * r)
                if n == 1:
                    pool.wait_ge(rows_done, 2)
                if n >= 2:
                    pool.wait_ge(scattered, 32 * (r - 1))
                pool.nop(nofuse=True)
                pool.tensor_copy(to_now[0:SW, par, :], to_row[0:SW, bass.ds((r - 1) * 2, 2)]).then_inc(now, 1)
                pool.wait_ge(now, copies)
                if n == 1:
                    pool.wait_ge(stored, 16 * NT)
                pool.nop(nofuse=True)
                for h in range(2):
                    pool.indirect_dma_start(out, bass.IndirectOffsetOnAxis(ap=to_now[0:SW, par, h:h + 1], axis=0),
                                            y[par][0:SW, h, :], None, compute_op=ALU.add).then_inc(scattered, 16)

            def step(r, par, n):
                ahead = r + 3
                if n <= TILES - 3:
                    pool.wait_ge(tT_ps, 2 * r + 2)
                    pool.wait_ge(cw_cmp_done, r + 1)
                    pool.nop(nofuse=True)
                    gather(ahead, 1 - par, ahead - 3 + (r - 3 if n >= 3 else 0))
                else:
                    ahead = TILES
                if n >= 3:
                    scatter(r - 2, par, n - 2, ahead - 3 + r - 2)
                for c in range(IC):
                    pool.wait_ge(tz_hi_done, 2 * (r - 1) + c + 1)
                    pool.tensor_tensor(tz_lo[par][:, c, :], tz32[:, c, :], tz_hi[par][:, c, :],
                                       ALU.subtract).then_inc(tz_split, 1)

            pool.wait_ge(rows_done, 1)
            pool.wait_ge(h_stored, 64)
            for r in (1, 2, 3):
                if r == 3:
                    pool.wait_ge(tT_ps, 2)
                    pool.wait_ge(cw_cmp_done, 1)
                gather_rows(r % 2, from_row[:, 2 * (r - 1):2 * r])
            rounds(pool, step)
            for r in (TILES - 1, TILES):
                scatter(r, r % 2, r, TILES - 3 + r)

        @block.scalar
        def _(act):
            act.preload_act_table_set("natural_log_exp_and_others")
            act.dma_start(mask_sb[0:S, :], mask).then_inc(mask_in, 16)
            act.dma_start(mask_sb[S:P, :], mask).then_inc(mask_in, 16)
            act.dma_start(norm_sb[:, :], qk_norm).then_inc(small_in, 16)
            act.dma_start(gate_st[:, :, :], gate_t.rearrange("p (k e) -> p k e", k=KC)).then_inc(small_in, 16)
            act.dma_start(bias_sb[:, :], bias).then_inc(small_in, 16)

            def ln_rstd(count, n):
                act.wait_ge(var_ready, count)
                act.activation(lnvar[:, n], lnvar[:, n], ACT.Ln, bias=eps_ln[:, :]).then_inc(lnvar_ready, 1)
                act.wait_ge(lnvar_ready, count)
                act.activation(rstd[:, n], lnvar[:, n], ACT.Exp, scale=-0.5).then_inc(rstd_ready, 1)

            act.wait_ge(consts, 14)
            act.activation(ident16[:, :], ident[:, :], ACT.Copy).then_inc(masks16, 1)
            act.activation(blockmask16[:, :], blockmask[:, :], ACT.Copy).then_inc(masks16, 1)

            def normalise_rows(count, dst, done):
                act.wait_ge(shift_ready, count)
                for n in ACT_ROWS:
                    act.activation(dst(n), xh[:, n, :], ACT.Identity, scale=rstd[:, n:n + 1],
                                   bias=shift_ln[:, n:n + 1]).then_inc(done, 1)

            ln_rstd(1, slice(0, B))
            normalise_rows(1, lambda n: hq[:, :, n], h1_act)
            act.wait_ge(ctx_in, 16)
            for c in range(KC):
                act.activation(ctx_hi[:, c, :], ctx_st[:, c, :], ACT.Copy).then_inc(ctx_hi_done, 1)

            def wq_chunk(c):
                act.activation(wq_hi[:, c, :], wq_st[:, c, :], ACT.Copy, scale=WS).then_inc(wq_hi_done, 1)

            def wkv_chunk(c):
                act.activation(wkv_hi[:, 2 * c:2 * c + 2, :], wkv_st[:, 2 * c:2 * c + 2, :], ACT.Copy,
                               scale=WS).then_inc(wkv_hi_done, 1)

            def first_exp(b):
                act.wait_ge(s1_shift, b + 1)
                act.activation(e1[:, b, :], e1[:, b, :], ACT.Exp, scale=float(S) ** -0.5).then_inc(e1_done, 1)

            def first_qT(t):
                act.wait_ge(qT1_ps, t + 1)
                act.activation(qT1[:, 4 * t:4 * t + 4, :], ps[:, 4 + t % 4, :].rearrange("p (j c) -> p j c", c=P),
                               ACT.Copy).then_inc(qT1_done, 1)

            def first_diag(b):
                act.wait_ge(p1_done, b + 1)
                act.wait_ge(diag_zero, 4)
                for k in range(4):
                    rows = slice(32 * k, 32 * k + 32)
                    act.activation(p1_diag[b][rows, :, rows], p1T[rows, b, :].rearrange("p (j m) -> p j m", m=32),
                                   ACT.Copy).then_inc(diag_done, 1)

            first_exp(0)
            first_exp(1)
            for t in range(4):
                first_qT(t)
            first_diag(0)
            first_exp(2)
            for t in range(4, 8):
                first_qT(t)
            first_diag(1)
            first_exp(3)
            first_diag(2)
            first_diag(3)

            def scale_staged(w):
                act.activation(w, w, ACT.Copy, scale=WS).then_inc(weights_scaled, 1)

            act.wait_ge(wkv_in, 16)
            for c in range(2):
                wkv_chunk(c)
                scale_staged(wkv_st[:, 2 * c:2 * c + 2, :])
            act.wait_ge(wq_in, 16)
            for c in range(KC):
                wq_chunk(c)
                scale_staged(wq_st[:, c, :])
            act.wait_ge(small_in, 48)
            act.activation(gate_hi[:, :, :], gate_st[:, :, :], ACT.Copy, scale=WS)
            scale_staged(gate_st[:, :, :])

            def transposed_hi(base, t, bank):
                act.wait_ge(hT_ps, base + t + 1)
                act.activation(hT_hi[:, :, t * P:(t + 1) * P], ps[:, bank, :].rearrange("p (k c) -> p k c", c=P),
                               ACT.Copy).then_inc(hT_hi_done, 1)

            def q_parts(p, u):
                j, th = u // 2, u % 2
                bank = ps[:, 4 + u % 2, :]
                act.wait_ge(q_ps, ev(p, 8, u))
                act.activation(q_hi[:, j // 2, 8 * th:8 * th + 8, j % 2, :],
                               bank.rearrange("p (b s) -> p b s", s=S), ACT.Copy).then_inc(q_hi_done, 1)
                if u >= 2:
                    act.wait_ge(sq_split, ev(p, 8, u - 2))
                act.activation(sq32[:, u % 2, :], bank, ACT.Square, scale=4.0 / WS).then_inc(sq32_done, 1)
                act.wait_ge(sq32_done, ev(p, 8, u))
                act.activation(sq_hi[:, j // 2, 8 * th:8 * th + 8, j % 2, :],
                               sq32[:, u % 2, :].rearrange("p (b s) -> p b s", s=S),
                               ACT.Copy).then_inc(sq_hi_done, 1)

            def soft_exp(i, b):
                act.wait_ge(shifted, ev(i, 4, b))
                act.activation(prob[:, b, :], prob[:, b, :], ACT.Exp).then_inc(exp_done, 1)

            def probs_hi(i, t):
                act.wait_ge(pT_ps, ev(i, NT, t))
                act.activation(pT_hi[:, t, :], ps[:, 6 + t % 2, 0:256], ACT.Copy).then_inc(pT_hi_done, 1)

            def heads_hi(i, t):
                act.wait_ge(pv_ps, ev(i, NT, t))
                act.activation(o_hi[:, :, t, :, :].rearrange("p h b s -> p b h s"),
                               ps[:, 0:2, 0:256].rearrange("p b (h s) -> p b h s", s=S),
                               ACT.Copy).then_inc(o_hi_done, 1)

            def k_parts(p, th):
                act.wait_ge(k_ps, ev(p, 2, th))
                act.activation(k32[:, th, :], ps[:, 4 + th, :], ACT.Copy, scale=1.0 / WS).then_inc(k32_done, 1)
                act.activation(ksq32[:, th, :], ps[:, 4 + th, :], ACT.Square, scale=4.0 / WS).then_inc(ksq32_done, 1)
                act.wait_ge(ksq32_done, ev(p, 2, th))
                act.activation(ksq_hi[:, th, :], ksq32[:, th, :], ACT.Copy).then_inc(ksq_hi_done, 1)

            def k_scale(p, th, bank):
                act.wait_ge(ssq_k_ps, ev(p, 2, th))
                act.activation(rk[:, th, :], ps[:, bank, :], ACT.Ln, scale=1.0 / (16 * HD),
                               bias=eps_ln[:, :]).then_inc(ln_k, 1)
                act.wait_ge(ln_k, ev(p, 2, th))
                act.activation(rk[:, th, :], rk[:, th, :], ACT.Exp, scale=-0.5).then_inc(rk_done, 1)

            def k_hi_part(p, th):
                act.wait_ge(k_norm, ev(p, 2, th))
                act.activation(k_hi[:, th * BANK:(th + 1) * BANK], k32[:, th, :], ACT.Copy).then_inc(k_hi_done, 1)

            def q_rms(p, bank):
                act.wait_ge(ssq_q_ps, p + 1)
                act.activation(rq[:, :], ps[:, bank, 0:32], ACT.Ln, scale=WS * WS / 16, bias=eps_q[:, :]).then_inc(ln_q, 1)
                act.wait_ge(ln_q, p + 1)
                act.activation(rq[:, :], rq[:, :], ACT.Exp, scale=-0.5).then_inc(rq_done, 1)

            def v_hi_part(p, th, bank):
                act.wait_ge(v_ps, ev(p, 2, th))
                act.activation(v_hi[:, 4 * th:4 * th + 4, :], ps[:, bank, :].rearrange("p (t d) -> p t d", d=HD),
                               ACT.Copy).then_inc(v_hi_done, 1)

            def expert_weights_hi(r, par, c):
                if c == 0:
                    act.wait_ge(wgu_in[par], loaded(r, par))
                act.activation(wgu_hi[par][:, c, :], wgu_st[par][:, c, :], ACT.Copy, scale=WS).then_inc(wgu_hi_done, 1)

            def down_weights_hi(r, par, c):
                if c == 0:
                    act.wait_ge(wd_in[par], loaded(r, par))
                act.activation(wd_hi[par][:, c, :], wd_st[par][:, c, :], ACT.Copy, scale=WS).then_inc(wd_hi_done, 1)

            def out_weights_hi(i, c, hi):
                if c == 0:
                    act.wait_ge(wo_in, 16 * i + 16)
                act.activation(hi[:, c, :], wo_st[:, c, :], ACT.Copy, scale=WS).then_inc(wo_hi_done, 1)

            def iteration(i, att, proj, split):
                p = i + 1
                for k in range(8):
                    if att and proj and k == 7:
                        probs_hi(i, 0)
                        probs_hi(i, 1)
                    if proj:
                        q_parts(p, k)
                    if not att:
                        if k == 1:
                            k_scale(p, 1, 7)
                        if k in (3, 4):
                            k_hi_part(p, k - 3)
                        if k == 7:
                            v_hi_part(p, 1, 7)
                    if att and 1 <= k < 5:
                        soft_exp(i, k - 1)
                    if att and proj and k >= 4:
                        out_weights_hi(i, k - 4, wo_hi)
                    if att and not proj and k < 2:
                        v_hi_part(i, k, 4 + k)
                    if att and not proj and k == 2:
                        probs_hi(i, 0)
                        probs_hi(i, 1)
                    if att and not proj and k == 3:
                        heads_hi(i, 0)
                if att and proj:
                    k_parts(p, 0)
                    heads_hi(i, 0)
                    k_parts(p, 1)
                    probs_hi(i, 2)
                    heads_hi(i, 1)
                if att and proj:
                    k_scale(p, 0, 4)
                for t in range(NT if att or split else 0):
                    if att and t + 2 < NT and not (proj and t == 0):
                        probs_hi(i, t + 2)
                    if att and proj and not split and t < HG:
                        out_weights_hi(G - 1, t, wq_hi)
                    if att and proj and t in (3, 4):
                        k_hi_part(p, t - 3)
                    if not proj and t == 0:
                        act.wait_ge(o_ps, NT * i)
                    if not proj and t < KC:
                        expert_weights_hi(0, 0, t)
                    if not proj and KC <= t < KC + IC:
                        down_weights_hi(0, 0, t - KC)
                    if att and t + 1 < NT and not (proj and t == 0):
                        heads_hi(i, t + 1)
                    if att and proj and t == 5:
                        q_rms(p, 4)
                    if split and 1 <= t < 1 + KC:
                        if t == 1:
                            act.wait_ge(wq_in, 16 * (i + 3))
                        wq_chunk(t - 1)
                    if att and proj and t == 0:
                        k_scale(p, 1, 5)
                    if split and att and t >= 6:
                        v_hi_part(p, t - 6, t - 2)
                    if not proj and t >= 1:
                        third_norm(t - 1)
                    if not proj and t >= 3:
                        transposed_hi(NT, t - 3, 4 + (t - 3) % 2)
                if not att:
                    q_rms(p, 3)
                if split:
                    act.wait_ge(wkv_in, 16 * (i + 3))
                    wkv_chunk(0)
                    wkv_chunk(1)

            def third_norm(t):
                ln_rstd(3 + t, slice(t, t + 1))

            k_parts(0, 0)
            k_parts(0, 1)
            ln_rstd(2, slice(0, B))
            normalise_rows(2, lambda n: h2[:, n, :], h2_act)
            for t in range(NT):
                transposed_hi(0, t, t % 4)
            v_hi_part(0, 0, 6)
            k_scale(0, 0, 7)
            iteration(-1, False, True, True)
            with act.Fori(0, G - 2) as i:
                iteration(i, True, True, True)
            iteration(G - 2, True, True, False)
            iteration(G - 1, True, False, False)
            third_norm(NT - 1)
            for t in range(NT - 3, NT):
                transposed_hi(NT, t, 4 + t % 2)

            act.wait_ge(logits, NT)
            act.activation(score[:, :, :], ps[:, 7, 0:NT * E].rearrange("p (t e) -> p t e", e=E), ACT.Exp,
                           scale=-1.0 / WS).then_inc(sig_exp, 1)

            def z_hi_part(u):
                act.wait_ge(z32_done, u + 1)
                c, th = u % 2, u // 2
                act.activation(z_hi[:, c, th * BANK:(th + 1) * BANK], z32[:, u % 2, :], ACT.Copy).then_inc(z_hi_done, 1)

            def shared_silu(u):
                act.wait_ge(gu_ps, u + 1)
                if u >= 2:
                    act.wait_ge(z32_done, u - 1)
                act.activation(silu[:, u % 2, :], ps[:, 2 * (u % 3), :], ACT.Silu, scale=1.0 / WS).then_inc(silu_done, 1)

            for u in range(3):
                shared_silu(u)
                if u >= 1:
                    z_hi_part(u - 1)
                if u == 2:
                    z_hi_part(2)
                    act.wait_ge(onehots, 1)
                    for t in range(NT):
                        ks = slice(t * TOPK, (t + 1) * TOPK)
                        act.activation(on_tok[:, ks, :], on_a[:, ks, :], ACT.Copy,
                                       scale=tok_no[:, t:t + 1]).then_inc(tokens_set, 1)
                        if t == NT // 2:
                            shared_silu(3)
            z_hi_part(3)

            def slots_hi(r, par):
                for j in range(2):
                    act.wait_ge(tT_ps, 2 * (r - 1) + j + 1)
                    act.activation(tT_hi[par][:, 2 * j:2 * j + 2, :],
                                   ps[:, 4 + j, 0:2 * TS].rearrange("p (k s) -> p k s", k=2),
                                   ACT.Copy).then_inc(tT_hi_done, 1)

            def gated(r, c):
                act.wait_ge(tgu_ps, 2 * (r - 1) + c + 1)
                act.activation(tsilu[:, c, :], ps[:, c, 0:TS], ACT.Silu, scale=1.0 / WS).then_inc(tsilu_done, 1)

            def gated_hi(r, par, c):
                act.wait_ge(tz32_done, 2 * (r - 1) + c + 1)
                act.activation(tz_hi[par][:, c, :], tz32[:, c, :], ACT.Copy).then_inc(tz_hi_done, 1)

            def weighted(r, par, n, h):
                act.wait_ge(td_ps, 2 * (r - 1) + h + 1)
                if h == 0:
                    act.wait_ge(cw_slot_done, r)
                    if n >= 3:
                        act.wait_ge(scattered, 32 * (r - 2))
                act.activation(y[par][0:SW, h, :], ps[0:SW, 6 + h, :], ACT.Copy,
                               scale=cw_slot[0:SW, par, h:h + 1]).then_inc(y_done, 1)

            def step(r, par, n):
                more = n < TILES
                if n == 1:
                    act.wait_ge(gu_ps, 4)
                    for c in range(KC):
                        expert_weights_hi(2, 0, c)
                    slots_hi(2, 0)
                elif more:
                    slots_hi(r + 1, 1 - par)
                    act.wait_ge(tgu_ps, 2 * (r - 1))
                    expert_weights_hi(r + 1, 1 - par, 0)
                    expert_weights_hi(r + 1, 1 - par, 1)
                gated(r, 0)
                if more and n > 1:
                    expert_weights_hi(r + 1, 1 - par, 2)
                gated_hi(r, par, 0)
                if more and n > 1:
                    expert_weights_hi(r + 1, 1 - par, 3)
                gated(r, 1)
                down_weights_hi(r, par, 0)
                gated_hi(r, par, 1)
                down_weights_hi(r, par, 1)
                if n >= 2:
                    for h in range(2):
                        weighted(r - 1, 1 - par, n - 1, h)

            for c in range(KC):
                expert_weights_hi(1, 1, c)
            slots_hi(1, 1)
            rounds(act, step)
            for h in range(2):
                weighted(TILES, TILES % 2, TILES, h)

        @block.vector
        def _(dve):
            steps = [0]

            def then(ins):
                steps[0] += 1
                ins.then_inc(chain, 1)
                dve.wait_ge(chain, steps[0])

            def half_rows(n):
                return dve.bn_stats(bnst[:, n, 0, :], xh[:, n, :])

            def joined(parts, rows):
                for n in rows:
                    last = dve.bn_aggr(mv[:, n, :], bnst[:, n, 0:parts, :])
                return last

            def row_scales(count, bank):
                dve.wait_ge(stats1, count)
                dve.wait_ge(swapped, count)
                other = ps[:, bank, 0:2 * B].rearrange("p (n s) -> p n s", s=2)
                dve.tensor_tensor(msum[:, :, :], mv[:, :, :], other, ALU.add)
                then(dve.tensor_tensor(mtmp[:, :], mv[:, :, 0], other[:, :, 0], ALU.subtract))
                then(dve.tensor_tensor(mtmp[:, :], mtmp[:, :], mtmp[:, :], ALU.mult))
                then(dve.scalar_tensor_tensor(lnvar[:, :], mtmp[:, :], 0.5, msum[:, :, 1], ALU.mult, ALU.add))
                dve.tensor_scalar(mean[:, :], msum[:, :, 0], 0.5, None, ALU.mult)
                dve.tensor_scalar(lnvar[:, :], lnvar[:, :], 0.5, None, ALU.mult).then_inc(var_ready, 1)

            for j in range(NT):
                dve.wait_ge(x_in[j], 16)
                for n in (2 * j, 2 * j + 1):
                    last = half_rows(n)
                if j >= 1:
                    joined(1, (2 * j - 2, 2 * j - 1))
                then(last)
            joined(1, (B - 2, B - 1)).then_inc(stats1, 1)
            dve.wait_ge(numbers, 7)
            dve.tensor_copy(count16[:, :], count_up[:, :])
            dve.tensor_scalar(below[:, :], count_up[:, :], row_no[:, 0:1], None, ALU.is_gt)
            dve.tensor_tensor(before[:, :, :], count_up[:, 0:E].unsqueeze(1).to_broadcast([P, E, E]),
                              count_up[:, 0:E].unsqueeze(2).to_broadcast([P, E, E]), ALU.is_lt)
            row_scales(1, 7)

            def normalise_rows(count, dst, done):
                dve.wait_ge(rstd_ready, count)
                dve.scalar_tensor_tensor(shift_ln[:, :], mean[:, :], -1.0, rstd[:, 0:B],
                                         ALU.mult, ALU.mult).then_inc(shift_ready, 1)
                for n in DVE_ROWS:
                    dve.tensor_scalar(dst(n), xh[:, n, :], mean[:, n:n + 1], rstd[:, n:n + 1],
                                      ALU.subtract, ALU.mult).then_inc(done, 1)

            normalise_rows(1, lambda n: hq[:, :, n], h1_dve)

            def wq_lo_chunk(c):
                dve.scalar_tensor_tensor(wq_lo[:, c, :], wq_st[:, c, :], WS, wq_hi[:, c, :],
                                         ALU.mult, ALU.subtract).then_inc(wq_split, 1)

            def wkv_lo_chunk(c):
                dve.scalar_tensor_tensor(wkv_lo[:, 2 * c:2 * c + 2, :], wkv_st[:, 2 * c:2 * c + 2, :], WS,
                                         wkv_hi[:, 2 * c:2 * c + 2, :], ALU.mult, ALU.subtract).then_inc(wkv_split, 1)

            def first_shift(b):
                dve.wait_ge(gram, b + 1)
                blocks = e1[:, b, :].rearrange("p (j m) -> p j m", m=32)
                masked_gram = ps[:, b, :].rearrange("p (j m) -> p j m", m=32)
                then(dve.tensor_reduce(smx[:, b, :], masked_gram, AX.X, ALU.max))
                dve.tensor_tensor(blocks, masked_gram, smx[:, b, :].unsqueeze(2).to_broadcast([P, 16, 32]),
                                  ALU.subtract).then_inc(s1_shift, 1)

            def first_probs(b):
                blocks = e1[:, b, :].rearrange("p (j m) -> p j m", m=32)
                dve.wait_ge(e1_done, b + 1)
                then(dve.tensor_reduce(ssum[:, b, :], blocks, AX.X, ALU.add))
                then(dve.reciprocal(sinv[:, b, :], ssum[:, b, :]))
                then(dve.tensor_tensor(blocks, blocks, sinv[:, b, :].unsqueeze(2).to_broadcast([P, 16, 32]), ALU.mult))
                dve.transpose(p1T[:, b, :], e1[:, b, :]).then_inc(p1_done, 1)

            first_shift(0)
            for b in range(1, 4):
                first_shift(b)
                first_probs(b - 1)
            first_probs(3)
            dve.wait_ge(x_plus_h, 4)
            xl = xh.rearrange("p n l -> p l n")
            for u in range(8):
                dve.wait_ge(msg, u + 1)
                part = xl[:, 32 * u:32 * u + 32, :]
                dve.tensor_tensor(part, part, ps[:, (u + 4) % 8, :].rearrange("p (l n) -> p l n", n=B),
                                  ALU.add).then_inc(x1_done, 1)
                if u == 3:
                    dve.wait_ge(x1_done, 4)
                    for n in range(B):
                        last = dve.bn_stats(bnst[:, n, 0, :], xh[:, n, 0:P])
            dve.wait_ge(x1_done, 8)
            for n in range(B):
                last = dve.bn_stats(bnst[:, n, 1, :], xh[:, n, P:2 * P])
            then(last)
            joined(2, range(B)).then_inc(stats1, 1)

            def transposed_lo(base, t, bank):
                dve.wait_ge(hT_hi_done, base + t + 1)
                dve.tensor_tensor(hT_lo[:, :, t * P:(t + 1) * P], ps[:, bank, :].rearrange("p (k c) -> p k c", c=P),
                                  hT_hi[:, :, t * P:(t + 1) * P], ALU.subtract).then_inc(hT_split, 1)

            def v_lo_part(p, th, bank):
                dve.wait_ge(v_hi_done, ev(p, 2, th))
                dve.tensor_tensor(v_lo[:, 4 * th:4 * th + 4, :], ps[:, bank, :].rearrange("p (t d) -> p t d", d=HD),
                                  v_hi[:, 4 * th:4 * th + 4, :], ALU.subtract).then_inc(v_split, 1)

            row_scales(2, 0)
            dve.wait_ge(small_in, 48)
            dve.tensor_tensor(wqk[:, :], norm_sb[:, 0:1], norm_sb[:, 1:2], ALU.mult).then_inc(dve_consts, 1)
            normalise_rows(2, lambda n: h2[:, n, :], h2_dve)
            for t in range(NT):
                transposed_lo(0, t, t % 4)
            v_lo_part(0, 0, 6)

            def q_lo_part(p, u):
                j, th = u // 2, u % 2
                dve.wait_ge(q_hi_done, ev(p, 8, u))
                dve.wait_ge(sq32_done, ev(p, 8, u))
                dve.tensor_tensor(q_lo[:, j // 2, 8 * th:8 * th + 8, j % 2, :],
                                  ps[:, 4 + u % 2, :].rearrange("p (b s) -> p b s", s=S),
                                  q_hi[:, j // 2, 8 * th:8 * th + 8, j % 2, :], ALU.subtract).then_inc(q_split, 1)

            def scale_scores(i, b):
                dve.wait_ge(s_ps, ev(i, 4, b))
                if b == 0:
                    dve.wait_ge(rq_done, i + 1)
                dve.tensor_tensor(prob[:, b, :].rearrange("p (g k) -> p g k", k=S),
                                  ps[:, b, :].rearrange("p (g k) -> p g k", k=S),
                                  rq[:, 8 * b:8 * b + 8].unsqueeze(2).to_broadcast([P, 8, S]),
                                  ALU.mult).then_inc(scaled, 1)

            def row_max(i, b):
                dve.wait_ge(masked, ev(i, 4, b))
                dve.tensor_reduce(rowmax[:, b, :], prob[:, b, :].rearrange("p (g k) -> p g k", k=S),
                                  AX.X, ALU.max).then_inc(max_done, 1)

            def normalise(i, b):
                t = prob[:, b, :].rearrange("p (g k) -> p g k", k=S)
                dve.wait_ge(exp_done, ev(i, 4, b))
                dve.tensor_reduce(rowsum[:, b, :], t, AX.X, ALU.add).then_inc(sum_done, 1)
                dve.wait_ge(sum_done, ev(i, 4, b))
                dve.reciprocal(rowinv[:, b, :], rowsum[:, b, :]).then_inc(inv_done, 1)
                dve.wait_ge(inv_done, ev(i, 4, b))
                dve.tensor_tensor(t, t, rowinv[:, b, :].unsqueeze(2).to_broadcast([P, 8, S]),
                                  ALU.mult).then_inc(prob_done, 1)

            def probs_lo(i, t):
                dve.wait_ge(pT_hi_done, ev(i, NT, t))
                dve.tensor_tensor(pT_lo[:, t, :], ps[:, 6 + t % 2, 0:256], pT_hi[:, t, :],
                                  ALU.subtract).then_inc(pT_split, 1)

            def heads_lo(i, t):
                dve.wait_ge(o_hi_done, ev(i, NT, t))
                dve.tensor_tensor(o_lo[:, :, t, :, :].rearrange("p h b s -> p b h s"),
                                  ps[:, 0:2, 0:256].rearrange("p b (h s) -> p b h s", s=S),
                                  o_hi[:, :, t, :, :].rearrange("p h b s -> p b h s"),
                                  ALU.subtract).then_inc(o_split, 1)

            def add_output(i, t):
                dve.wait_ge(o_ps, ev(i, NT, t))
                dve.scalar_tensor_tensor(x_res[:, t, :], ps[:, 2 + t % 2, :], 1.0 / (WS * WS), x_res[:, t, :],
                                         ALU.mult, ALU.add).then_inc(o_added, 1)

            def key_norm(p, th):
                dve.wait_ge(rk_done, ev(p, 2, th))
                dve.wait_ge(k32_done, ev(p, 2, th))
                if th == 0:
                    dve.wait_ge(dve_consts, 1)
                dve.scalar_tensor_tensor(k32[:, th, :], k32[:, th, :], wqk[:, 0:1], rk[:, th, :],
                                         ALU.mult, ALU.mult).then_inc(k_norm, 1)

            def key_lo(p, th):
                cols = slice(th * BANK, (th + 1) * BANK)
                dve.wait_ge(k_hi_done, ev(p, 2, th))
                dve.tensor_tensor(k_lo[:, cols], k32[:, th, :], k_hi[:, cols], ALU.subtract).then_inc(k_split, 1)

            def expert_weights_lo(r, par, c):
                dve.wait_ge(wgu_hi_done, KC * r + c + 1)
                dve.scalar_tensor_tensor(wgu_lo[par][:, c, :], wgu_st[par][:, c, :], WS, wgu_hi[par][:, c, :],
                                         ALU.mult, ALU.subtract).then_inc(wgu_split, 1)

            def down_weights_lo(r, par, c):
                dve.wait_ge(wd_hi_done, IC * r + c + 1)
                dve.scalar_tensor_tensor(wd_lo[par][:, c, :], wd_st[par][:, c, :], WS, wd_hi[par][:, c, :],
                                         ALU.mult, ALU.subtract).then_inc(wd_split, 1)

            def third_stats(t):
                dve.wait_ge(o_added, ev(G - 1, NT, t))
                then(dve.bn_stats(bnst[:, t, 0, :], x_res[:, t, :]))
                then(dve.bn_aggr(mv[:, t, :], bnst[:, t, 0:1, :]))
                dve.tensor_copy(lnvar[:, t:t + 1], mv[:, t, 1:2]).then_inc(var_ready, 1)

            def third_norm(t):
                dve.wait_ge(rstd_ready, 3 + t)
                dve.tensor_scalar(h_tok[:, t, :], x_res[:, t, :], mv[:, t, 0:1], rstd[:, t:t + 1],
                                  ALU.subtract, ALU.mult).then_inc(h_done, 1)

            def out_weights_lo(i, c, hi, lo):
                dve.wait_ge(wo_hi_done, ev(i, HG, c))
                dve.scalar_tensor_tensor(lo[:, c, :], wo_st[:, c, :], WS, hi[:, c, :],
                                         ALU.mult, ALU.subtract).then_inc(wo_split, 1)

            def iteration(i, att, proj, split):
                p = i + 1
                if att and proj:
                    for b in range(4):
                        scale_scores(i, b)
                for k in range(8 if proj else 0):
                    if att and k < 2:
                        row_max(i, 2 * k)
                        row_max(i, 2 * k + 1)
                    if att and k == 7:
                        probs_lo(i, 0)
                        probs_lo(i, 1)
                    q_lo_part(p, k)
                    if not att:
                        if k in (1, 2):
                            key_norm(p, k - 1)
                        if k in (4, 5):
                            key_lo(p, k - 4)
                        if k == 7:
                            v_lo_part(p, 1, 7)
                    if att and 2 <= k < 6:
                        normalise(i, k - 2)
                    if att and k >= 4:
                        out_weights_lo(i, k - 4, wo_hi, wo_lo)
                if not proj:
                    scale_scores(i, 0)
                    scale_scores(i, 1)
                    v_lo_part(i, 0, 4)
                    row_max(i, 0)
                    scale_scores(i, 2)
                    row_max(i, 1)
                    scale_scores(i, 3)
                    normalise(i, 0)
                    row_max(i, 2)
                    probs_lo(i, 0)
                    probs_lo(i, 1)
                    normalise(i, 1)
                    heads_lo(i, 0)
                    add_output(i - 1, NT - 2)
                    row_max(i, 3)
                    v_lo_part(i, 1, 5)
                    add_output(i - 1, NT - 1)
                    normalise(i, 2)
                elif att:
                    heads_lo(i, 0)
                for t in range(NT if att or split else 0):
                    if att and 1 <= t <= (NT if split or not proj else NT - LATE):
                        add_output(i, t - 1)
                        if not proj:
                            third_stats(t - 1)
                    if att and t + 2 < NT:
                        probs_lo(i, t + 2)
                    if att and t + 1 < NT:
                        heads_lo(i, t + 1)
                    if not proj and t == 1:
                        normalise(i, 3)
                    if att and proj and t in (1, 2):
                        key_norm(p, t - 1)
                    if split and 2 <= t < 2 + KC:
                        dve.wait_ge(wq_hi_done, ev(i + 2, KC, t - 2))
                        wq_lo_chunk(t - 2)
                    if att and proj and not split and 2 <= t < 2 + HG:
                        out_weights_lo(G - 1, t - 2, wq_hi, wq_lo)
                    if att and proj and t in (5, 6):
                        key_lo(p, t - 5)
                    if not proj and 1 <= t < 1 + KC:
                        expert_weights_lo(0, 0, t - 1)
                    if not proj and 1 + KC <= t < 1 + KC + IC:
                        down_weights_lo(0, 0, t - 1 - KC)
                    if att and split and t >= 6:
                        v_lo_part(p, t - 6, t - 2)
                    if not proj and t >= 2:
                        third_norm(t - 2)
                    if not proj and t >= 3:
                        transposed_lo(NT, t - 3, 4 + (t - 3) % 2)
                if att and (split or not proj):
                    add_output(i, NT - 1)
                if split:
                    for c in range(2):
                        dve.wait_ge(wkv_hi_done, ev(i + 2, 2, c))
                        wkv_lo_chunk(c)

            iteration(-1, False, True, True)
            dve.wait_ge(x1_moved, 64)
            with dve.Fori(0, G - 2) as i:
                iteration(i, True, True, True)
            iteration(G - 2, True, True, False)
            iteration(G - 1, True, False, False)
            third_stats(NT - 1)
            third_norm(NT - 2)
            transposed_lo(NT, NT - 3, 4 + (NT - 3) % 2)
            third_norm(NT - 1)
            transposed_lo(NT, NT - 2, 4 + (NT - 2) % 2)
            transposed_lo(NT, NT - 1, 4 + (NT - 1) % 2)

            def shared_z(u):
                dve.wait_ge(silu_done, u + 1)
                if u >= 2:
                    dve.wait_ge(z_split, u - 1)
                dve.scalar_tensor_tensor(z32[:, u % 2, :], ps[:, 2 * (u % 3) + 1, :], 1.0 / WS, silu[:, u % 2, :],
                                         ALU.mult, ALU.mult).then_inc(z32_done, 1)

            dve.wait_ge(sig_exp, 1)
            then(dve.tensor_scalar(score[:, :, :], score[:, :, :], 1.0, None, ALU.add))
            then(dve.reciprocal(score[:, :, :], score[:, :, :]))
            then(dve.tensor_tensor(score[:, :, :], score[:, :, :],
                                   bias_sb[:, :].unsqueeze(1).to_broadcast([P, NT, E]), ALU.add))
            for t in range(NT):
                last = dve.max(top8[:, t, :], score[:, t, :])
            then(last)
            then(dve.memset(top8[:, :, TOPK:8], -NEG))
            for t in range(NT):
                last = dve.match_replace(left[:, t, :], top8[:, t, :], score[:, t, :], NEG)
            then(last)
            dve.tensor_tensor(sel[:, :, :], left[:, :, :], score[:, :, :], ALU.not_equal).then_inc(sel_done, 1)
            shared_z(0)
            then(dve.tensor_reduce(wsum[:, :], top8[:, :, 0:TOPK], AX.X, ALU.add))
            then(dve.tensor_scalar(wsum[:, :], wsum[:, :], 1e-20, WS, ALU.add, ALU.mult))
            dve.wait_ge(sel_done, 1)
            dve.tensor_tensor(cw[:, :, :], sel[:, :, :], score[:, :, :], ALU.mult)
            then(dve.reciprocal(wsum[:, :], wsum[:, :]))
            dve.tensor_tensor(cw[:, :, :], cw[:, :, :], wsum[:, :].unsqueeze(2).to_broadcast([P, NT, E]),
                              ALU.mult).then_inc(cw_done, 1)

            dve.wait_ge(rank_ps, 1)
            rank = ps[:, 6, 0:NT * E].rearrange("p (t e) -> p t e", e=E)
            total = ps[:, 6, NT * E:(NT + 1) * E]
            then(dve.tensor_tensor(need[:, :, :], total.unsqueeze(2).to_broadcast([P, E, NJT]),
                                   tile_steps[:, :].unsqueeze(1).to_broadcast([P, E, NJT]), ALU.is_gt))
            then(dve.tensor_reduce(tiles[:, :], need[:, :, :], AX.X, ALU.add))
            then(dve.tensor_tensor(before[:, :, :], before[:, :, :],
                                   tiles[:, :].unsqueeze(1).to_broadcast([P, E, E]), ALU.mult))
            then(dve.tensor_reduce(first_tile[:, :], before[:, :, :], AX.X, ALU.add))
            dve.tensor_tensor(past_tile[:, :], first_tile[:, :], tiles[:, :], ALU.add)
            shared_z(1)
            then(dve.tensor_scalar(first_tile[:, :], first_tile[:, :], float(TS), 1.0, ALU.mult, ALU.add))
            then(dve.tensor_tensor(key[:, :, :], rank, first_tile[:, :].unsqueeze(1).to_broadcast([P, NT, E]), ALU.add))
            then(dve.tensor_tensor(key[:, :, :], key[:, :, :], sel[:, :, :], ALU.mult))
            for t in range(NT):
                last = dve.max(key8[:, t, :], key[:, t, :])
            then(last)
            then(dve.tensor_scalar(slot[:, :].rearrange("p (t k) -> p t k", k=TOPK), key8[:, :, 0:TOPK], -1.0, None,
                                   ALU.add))
            hi_cmp, lo_cmp = steps_cmp[:, :, :], steps_cmp[:, :, 0:HI8 - 1]
            then(dve.tensor_tensor(hi_cmp, slot[:, :].unsqueeze(2).to_broadcast([P, NTK, HI8]),
                                   hi_steps[:, :].unsqueeze(1).to_broadcast([P, NTK, HI8]), ALU.is_ge))
            then(dve.tensor_reduce(slot_hi[:, :], hi_cmp, AX.X, ALU.add))
            then(dve.scalar_tensor_tensor(slot_rest[:, :], slot_hi[:, :], -float(HI8 * SW), slot[:, :],
                                          ALU.mult, ALU.add))
            then(dve.tensor_tensor(lo_cmp, slot_rest[:, :].unsqueeze(2).to_broadcast([P, NTK, HI8 - 1]),
                                   lo_steps[:, :].unsqueeze(1).to_broadcast([P, NTK, HI8 - 1]), ALU.is_ge))
            then(dve.tensor_reduce(slot_lo[:, :], lo_cmp, AX.X, ALU.add))
            dve.scalar_tensor_tensor(slot_a[:, :], slot_hi[:, :], float(HI8), slot_lo[:, :], ALU.mult, ALU.add)
            then(dve.scalar_tensor_tensor(slot_b[:, :], slot_lo[:, :], -float(SW), slot_rest[:, :], ALU.mult, ALU.add))
            shared_z(2)
            dve.tensor_tensor(on_a, slot_a[:, :].unsqueeze(2).to_broadcast([P, NTK, NS]),
                              count16[:, 0:NS].unsqueeze(1).to_broadcast([P, NTK, NS]), ALU.is_equal).then_inc(onehots, 1)
            then(dve.tensor_tensor(tile_cmp[:, :, :], past_tile[:, :].unsqueeze(1).to_broadcast([P, TILES, E]),
                                   count_up[:, 0:TILES].unsqueeze(2).to_broadcast([P, TILES, E]), ALU.is_le))
            then(dve.tensor_reduce(eid[:, :], tile_cmp[:, :, :], AX.X, ALU.add))
            then(dve.tensor_scalar(eid[:, :], eid[:, :], float(E - 1), None, ALU.min))
            dve.tensor_copy(eid_int[:, :], eid[:, :]).then_inc(eid_done, 1)

            def second_onehot(cs):
                dve.tensor_tensor(on_b[:, cs, :], slot_b[:, cs].unsqueeze(2).to_broadcast([P, NTK // 2, SW]),
                                  count16[:, 0:SW].unsqueeze(1).to_broadcast([P, NTK // 2, SW]),
                                  ALU.is_equal).then_inc(onehots, 1)

            second_onehot(slice(0, NTK // 2))
            shared_z(3)
            second_onehot(slice(NTK // 2, NTK))
            dve.wait_ge(eid_done, 1)
            then(dve.tensor_tensor(is_eid[:, :, :], eid[:, :].unsqueeze(2).to_broadcast([P, TILES, E]),
                                   count_up[:, 0:E].unsqueeze(1).to_broadcast([P, TILES, E]), ALU.is_equal))

            def shared_add(t):
                dve.wait_ge(d_ps, t + 1)
                dve.scalar_tensor_tensor(x_res[:, t, :], ps[:, down_bank[t], :], 1.0 / WS, x_res[:, t, :],
                                         ALU.mult, ALU.add).then_inc(d_added, 1)

            dve.wait_ge(slot_ps, 1)
            dve.tensor_scalar(from_row[0:SW, :], ps[0:SW, 7, 0:NS], float(T), float(T - 1),
                              ALU.add, ALU.min).then_inc(rows_done, 1)
            then(dve.scalar_tensor_tensor(dump[0:SW, :], ps[0:SW, 7, 0:NS], 0.0, dump_no[0:SW, :],
                                          ALU.is_equal, ALU.mult))
            dve.scalar_tensor_tensor(to_row[0:SW, :], ps[0:SW, 7, 0:NS], float(T), dump[0:SW, :],
                                     ALU.add, ALU.add).then_inc(rows_done, 1)
            for c in range(KC):
                shared_add(add_order[c])
                if c >= 2:
                    expert_weights_lo(1, 1, 2 * c - 4)
                    expert_weights_lo(1, 1, 2 * c - 3)

            def slots_lo(r, par):
                for j in range(2):
                    dve.wait_ge(tT_hi_done, 2 * (r - 1) + j + 1)
                    dve.tensor_tensor(tT_lo[par][:, 2 * j:2 * j + 2, :],
                                      ps[:, 4 + j, 0:2 * TS].rearrange("p (k s) -> p k s", k=2),
                                      tT_hi[par][:, 2 * j:2 * j + 2, :], ALU.subtract).then_inc(tT_split, 1)

            def gated_up(r, n, c):
                dve.wait_ge(tsilu_done, 2 * (r - 1) + c + 1)
                if n >= 2:
                    dve.wait_ge(tz_split, 2 * (r - 2) + c + 1)
                dve.scalar_tensor_tensor(tz32[:, c, :], ps[:, c, 256:256 + TS], 1.0 / WS, tsilu[:, c, :],
                                         ALU.mult, ALU.mult).then_inc(tz32_done, 1)

            def slot_weights(r, par):
                dve.wait_ge(gathered[par], slots_read(r, par))
                dve.tensor_tensor(cw_cmp[0:SW, par, :, :], h_slot[par][0:SW, :, D:HROW],
                                  is_eid[0:SW, bass.ds(r - 1, 1), :].to_broadcast([SW, 2, E]),
                                  ALU.mult).then_inc(cw_cmp_done, 1)

            def slot_weights_sum(r, par, n):
                dve.wait_ge(cw_cmp_done, r)
                if n >= 3:
                    dve.wait_ge(y_done, 2 * (r - 2))
                dve.tensor_reduce(cw_slot[0:SW, par, :], cw_cmp[0:SW, par, :, :], AX.X, ALU.add).then_inc(cw_slot_done, 1)

            def step(r, par, n):
                more = n < TILES
                if n == 1:
                    for c in range(KC):
                        expert_weights_lo(2, 0, c)
                if more:
                    slots_lo(r + 1, 1 - par)
                    slot_weights(r + 1, 1 - par)
                if more and n > 1:
                    expert_weights_lo(r + 1, 1 - par, 0)
                    expert_weights_lo(r + 1, 1 - par, 1)
                gated_up(r, n, 0)
                if more and n > 1:
                    expert_weights_lo(r + 1, 1 - par, 2)
                    expert_weights_lo(r + 1, 1 - par, 3)
                gated_up(r, n, 1)
                for c in range(IC):
                    down_weights_lo(r, par, c)
                if more:
                    slot_weights_sum(r + 1, 1 - par, n + 1)

            slot_weights(1, 1)
            slots_lo(1, 1)
            slot_weights_sum(1, 1, 1)
            for t in add_order[KC:]:
                shared_add(t)
            rounds(dve, step)

        @block.tensor
        def _(pe):
            def product(dst, terms, chunks):
                n = len(terms) * len(chunks)
                m = 0
                for c in chunks:
                    for lhsT, rhs in terms:
                        last = pe.matmul(dst, lhsT(c), rhs(c), start=(m == 0), stop=(m == n - 1))
                        m += 1
                return last

            def parts(lhs_hi, lhs_lo, rhs_hi, rhs_lo):
                return [(lhs_hi, rhs_hi), (lhs_hi, rhs_lo), (lhs_lo, rhs_hi)]

            pe.wait_ge(consts, 14)
            pe.wait_ge(masks16, 2)

            def keep_clock(n):
                for _ in range(n):
                    pe.matmul(ps[:, 4, :].rearrange("p (j m) -> p j m", m=32), ident16[:, :],
                              blockmask16[:, :].unsqueeze(1).to_broadcast([P, 16, 32]), start=True, stop=True)

            keep_clock(12)
            pe.wait_ge(stats1, 1)
            pe.matmul(ps[:, 7, 0:2 * B], swap[:, :], mv[:, :, :].rearrange("p n s -> p (n s)"),
                      start=True, stop=True).then_inc(swapped, 1)
            keep_clock(27)
            pe.wait_ge(h1_dve, len(DVE_ROWS))
            pe.wait_ge(h1_act, len(ACT_ROWS))

            def gram_bank(jh, half):
                b = 2 * jh + half
                rows = slice(half * S, half * S + S)

                def add_mask(start, stop):
                    return pe.matmul(ps[:, b, :].rearrange("p (j m) -> p j m", m=32), ident16[:, :],
                                     blockmask16[:, :].unsqueeze(1).to_broadcast([P, 16, 32]), start=start, stop=stop)

                add_mask(start=True, stop=False)
                for j in range(16):
                    for k in range(4):
                        l0 = LG * (16 * jh + j) + 2 * k
                        q2 = hq[rows, l0:l0 + 2, :].rearrange("p l n -> p (l n)")
                        pe.matmul(ps[32 * k:32 * k + 32, b, 32 * j:32 * j + 32], q2, q2, start=False, stop=False)
                add_mask(start=False, stop=True).then_inc(gram, 1)

            def first_transposes(t):
                if t >= 4:
                    pe.wait_ge(qT1_done, t - 3)
                for j in range(4):
                    l0 = LG * (4 * t + j)
                    last = pe.transpose(ps[:, 4 + t % 4, j * P:(j + 1) * P],
                                        hq[:, l0:l0 + LG, :].rearrange("p l n -> p (l n)"), ident[:, :])
                last.then_inc(qT1_ps, 1)

            gram_bank(0, 0)
            gram_bank(0, 1)
            pe.wait_ge(var_ready, 1)
            for t in range(4):
                first_transposes(t)
            gram_bank(1, 0)
            for t in range(4, 8):
                first_transposes(t)
            gram_bank(1, 1)
            pe.wait_ge(qT1_done, 8)
            for jh in range(2):
                pe.wait_ge(diag_done, 8 * jh + 8)
                if jh == 1:
                    pe.wait_ge(s1_shift, 4)
                for u in range(4):
                    for half in range(2):
                        for j in range(4 * u, 4 * u + 4):
                            last = pe.matmul(ps[half * S:half * S + S, 4 * (1 - jh) + u, (j % 4) * P:(j % 4 + 1) * P],
                                             qT1[:, 16 * jh + j, half * S:half * S + S],
                                             p1_diag[2 * jh + half][:, j, :], start=True, stop=True)
                    last.then_inc(msg, 1)

            def transpose_rows(t):
                pe.wait_ge(h2_dve, rows_to(DVE_ROWS, 2 * t + 1))
                pe.wait_ge(h2_act, rows_to(ACT_ROWS, 2 * t + 1))
                if t >= 4:
                    pe.wait_ge(hT_split, t - 3)
                cols = ps[:, t % 4, :].rearrange("p (h k b c) -> p k b h c", h=2, k=2, b=2)
                for b in range(2):
                    for k in range(2):
                        last = pe.transpose(cols[:, k, b, :, :], h2[:, 2 * t + b, k * P:(k + 1) * P], ident[:, :])
                last.then_inc(hT_ps, 1)

            def transpose_tokens(t, bank):
                pe.wait_ge(h_done, t + 1)
                if t >= 2:
                    pe.wait_ge(hT_split, NT + t - 1)
                for c in range(KC):
                    last = pe.transpose(ps[:, bank, c * P:(c + 1) * P], h_tok[:, t, c * P:(c + 1) * P], ident[:, :])
                last.then_inc(hT_ps, 1)

            def scores(i, b):
                if b == 0:
                    pe.wait_ge(q_split, 8 * i + 8)
                    pe.wait_ge(k_split, 2 * i + 2)
                for t in range(2):
                    for m in range(2):
                        for r in range(2):
                            n = 2 * (2 * b + t) + r
                            col = ((t * 2 + m) * 2 + r) * S
                            last = product(
                                ps[:, b, col:col + S],
                                parts(lambda _: q_hi[:, m, n, :, :].rearrange("p h s -> p (h s)"),
                                      lambda _: q_lo[:, m, n, :, :].rearrange("p h s -> p (h s)"),
                                      lambda _: k_hi[:, n * S:(n + 1) * S],
                                      lambda _: k_lo[:, n * S:(n + 1) * S]), [0])
                last.then_inc(s_ps, 1)

            def project_q(p, u):
                j, th = u // 2, u % 2
                if u == 0:
                    pe.wait_ge(wq_split, p * KC + KC)
                if u >= 2:
                    pe.wait_ge(q_split, ev(p, 8, u - 2))
                cols = slice(th * BANK, (th + 1) * BANK)
                heads = slice(j * HD, (j + 1) * HD)
                product(ps[:, 4 + u % 2, :],
                        parts(lambda c: wq_hi[:, c, heads], lambda c: wq_lo[:, c, heads],
                              lambda c: hT_hi[:, c, cols], lambda c: hT_lo[:, c, cols]),
                        range(KC)).then_inc(q_ps, 1)

            def project_k(p, th):
                if th == 0:
                    pe.wait_ge(wkv_split, p * 2 + 2)
                cols = slice(th * BANK, (th + 1) * BANK)
                product(ps[:, 4 + th, :],
                        parts(lambda c: wkv_hi[:, c, 0:HD], lambda c: wkv_lo[:, c, 0:HD],
                              lambda c: ctx_hi[:, c, cols], lambda c: ctx_lo[:, c, cols]),
                        range(KC)).then_inc(k_ps, 1)

            def project_v(p, th, bank, tiles=range(4)):
                for t in range(4 * th + tiles[0], 4 * th + tiles[-1] + 1):
                    rows = slice(t * P, (t + 1) * P)
                    last = product(ps[:, bank, (t % 4) * HD:(t % 4 + 1) * HD],
                                   parts(lambda c: ctx_hi[:, c, rows], lambda c: ctx_lo[:, c, rows],
                                         lambda c: wkv_hi[:, c, HD:2 * HD], lambda c: wkv_lo[:, c, HD:2 * HD]),
                                   range(KC))
                if tiles[-1] == 3:
                    last.then_inc(v_ps, 1)

            def sum_q_squares(p, bank, tiles=range(NT)):
                pe.wait_ge(sq_split, 8 * p + (7 if tiles[-1] < NT // 2 else 8))
                for t in tiles:
                    for m in range(2):
                        for r in range(2):
                            col = (t * 2 + m) * 2 + r
                            for n, part in enumerate((sq_hi, sq_lo)):
                                last = pe.matmul(ps[:, bank, col:col + 1],
                                                 part[:, m, 2 * t + r, :, :].rearrange("p h s -> p (h s)"),
                                                 ones[:, 0:1], start=(n == 0), stop=(n == 1))
                if tiles[-1] == NT - 1:
                    last.then_inc(ssq_q_ps, 1)

            def sum_k_squares(p, th, bank):
                pe.wait_ge(ksq_split, ev(p, 2, th))
                pe.matmul(ps[:, bank, :], ones[:, :], ksq_hi[:, th, :], start=True, stop=False)
                pe.matmul(ps[:, bank, :], ones[:, :], ksq_lo[:, th, :], start=False, stop=True).then_inc(ssq_k_ps, 1)

            def transpose_probs(i, t):
                b = t // 2
                if t % 2 == 0:
                    pe.wait_ge(prob_done, ev(i, 4, b))
                if t >= 2:
                    pe.wait_ge(pT_split, ev(i, NT, t - 2))
                for m in range(2):
                    col = ((t % 2) * 2 + m) * P
                    last = pe.transpose(ps[:, 6 + t % 2, m * P:(m + 1) * P], prob[:, b, col:col + P], ident[:, :])
                last.then_inc(pT_ps, 1)

            def heads_out(i, t):
                pe.wait_ge(pT_split, ev(i, NT, t))
                if t == 0:
                    pe.wait_ge(scaled, 4 * i + 4)
                else:
                    pe.wait_ge(o_split, ev(i, NT, t - 1))
                for n, (v, pt) in enumerate(((v_hi, pT_hi), (v_hi, pT_lo), (v_lo, pT_hi))):
                    for r in range(2):
                        rows = slice(r * S, (r + 1) * S)
                        last = pe.matmul(ps[:, r, 0:256], v[rows, t, :], pt[rows, t, :],
                                         start=(n == 0), stop=(n == 2))
                last.then_inc(pv_ps, 1)

            def output(i, t, hi, lo):
                pe.wait_ge(o_split, ev(i, NT, t))
                if t == 0:
                    pe.wait_ge(wo_split, HG * i + HG)
                if t >= 2:
                    pe.wait_ge(o_added, ev(i, NT, t - 2))
                product(ps[:, 2 + t % 2, :],
                        parts(lambda h: o_hi[:, h, t, :, :].rearrange("p b s -> p (b s)"),
                              lambda h: o_lo[:, h, t, :, :].rearrange("p b s -> p (b s)"),
                              lambda h: hi[:, h, :], lambda h: lo[:, h, :]),
                        range(HG)).then_inc(o_ps, 1)

            def iteration(i, att, proj, first=False, values=True):
                p = i + 1
                if att and not proj:
                    pe.wait_ge(ln_k, ev(i, 2, 1))
                    pe.wait_ge(ln_q, i + 1)
                    project_v(i, 0, 4)
                    pe.wait_ge(o_split, i * NT)
                if att:
                    for b in range(4):
                        if not first and b >= 2:
                            pe.wait_ge(o_added, i * NT + (b - 3) - (0 if proj else LATE))
                        if first and b == 3:
                            pe.wait_ge(ln_q, 1)
                        scores(i, b)
                        if first and b == 0:
                            sum_q_squares(i, 3, range(NT // 2, NT))
                if proj:
                    for u in range(8):
                        if u < 2:
                            if att:
                                pe.wait_ge(v_split, ev(i, 2, u))
                            else:
                                pe.wait_ge(hT_split, 4 * u + 4)
                        if att and u == 7:
                            if first:
                                pe.wait_ge(v_split, 2)
                            transpose_probs(i, 0)
                            transpose_probs(i, 1)
                        project_q(p, u)
                        if not att and u == 0:
                            pe.wait_ge(ln_k, 1)
                            sum_k_squares(p, 1, 7)
                    if att:
                        pe.wait_ge(q_split, ev(p, 8, 6))
                        project_k(p, 0)
                        heads_out(i, 0)
                        pe.wait_ge(q_split, ev(p, 8, 7))
                        project_k(p, 1)
                        transpose_probs(i, 2)
                        sum_k_squares(p, 0, 4)
                    else:
                        pe.wait_ge(ln_k, 2)
                        project_v(p, 1, 7)
                        sum_q_squares(p, 3, range(NT // 2))
                if att and not proj:
                    project_v(i, 1, 5)
                    pe.wait_ge(scaled, 4 * i + 3)
                    output(i - 1, NT - 2, wo_hi, wo_lo)
                    transpose_probs(i, 0)
                    transpose_probs(i, 1)
                    heads_out(i, 0)
                    pe.wait_ge(scaled, 4 * i + 4)
                    output(i - 1, NT - 1, wo_hi, wo_lo)
                if att:
                    for t in range(NT):
                        if t + 2 < NT and not (proj and t == 0):
                            transpose_probs(i, t + 2)
                        if t + 1 < NT:
                            heads_out(i, t + 1)
                        if proj and values and t >= 6:
                            pe.wait_ge(ln_k, ev(p, 2, t - 6))
                            if t == 6:
                                pe.wait_ge(ln_q, p + 1)
                            project_v(p, t - 6, t - 2)
                        if not proj and t < 2:
                            pe.wait_ge(o_added, ev(i - 1, NT, NT - LATE + t))
                        if values or t < NT - LATE:
                            output(i, t, *((wo_hi, wo_lo) if proj else (wq_hi, wq_lo)))
                        if not proj and t >= 3:
                            transpose_tokens(t - 3, 4 + (t - 3) % 2)
                        if proj and t == 0:
                            sum_k_squares(p, 1, 5)
                        if proj and 1 <= t <= 4:
                            if t == 1:
                                pe.wait_ge(ln_k, ev(p, 2, 0))
                            sum_q_squares(p, 4, range(2 * t - 2, 2 * t))

            pe.wait_ge(ctx_split, KC)
            for th in range(2):
                pe.wait_ge(x1_done, th + 1)
                project_k(0, th)
            pe.wait_ge(x1_done, 3)
            project_v(0, 0, 6, range(2))
            pe.wait_ge(stats1, 2)
            pe.matmul(ps[:, 0, 0:2 * B], swap[:, :], mv[:, :, :].rearrange("p n s -> p (n s)"),
                      start=True, stop=True).then_inc(swapped, 1)
            project_v(0, 0, 6, range(2, 4))
            pe.wait_ge(var_ready, 2)
            sum_k_squares(0, 0, 7)
            for t in range(NT):
                transpose_rows(t)
            iteration(-1, False, True)
            iteration(0, True, True, first=True)
            with pe.Fori(1, G - 2) as i:
                iteration(i, True, True)
            iteration(G - 2, True, True, values=False)
            iteration(G - 1, True, False)

            def shared_unit(u):
                if u == 0:
                    pe.wait_ge(wgu_split, KC)
                    pe.wait_ge(hT_split, NT + 4)
                if u == 2:
                    pe.wait_ge(hT_split, 2 * NT)
                if u == 1:
                    pe.wait_ge(o_added, NT * G)
                if u == 3:
                    pe.wait_ge(z32_done, 1)
                c, th = u % 2, u // 2
                cols = slice(th * BANK, (th + 1) * BANK)
                for gu in range(2):
                    w = slice(gu * I + c * P, gu * I + (c + 1) * P)
                    last = product(ps[:, 2 * (u % 3) + gu, :],
                                   parts(lambda k: wgu_hi[0][:, k, w], lambda k: wgu_lo[0][:, k, w],
                                         lambda k: hT_hi[:, k, cols], lambda k: hT_lo[:, k, cols]), range(KC))
                    if u == 0 and gu == 0:
                        transpose_tokens(NT - 3, 4 + (NT - 3) % 2)
                last.then_inc(gu_ps, 1)

            def route(t):
                if t == 0:
                    pe.wait_ge(gate_split, 1)
                pe.wait_ge(hT_split, NT + t + 1)
                rows = slice(t * P, (t + 1) * P)
                product(ps[:, 7, t * E:(t + 1) * E],
                        parts(lambda c: hT_hi[:, c, rows], lambda c: hT_lo[:, c, rows],
                              lambda c: gate_hi[:, c, :], lambda c: gate_lo[:, c, :]), range(KC)).then_inc(logits, 1)

            shared_unit(0)
            transpose_tokens(NT - 2, 4 + (NT - 2) % 2)
            transpose_tokens(NT - 1, 4 + (NT - 1) % 2)
            for t in range(NT):
                route(t)

            def shared_down(t):
                pe.wait_ge(z_split, 2 if t < 4 else 4)
                if t == 0:
                    pe.wait_ge(wd_split, IC)
                if t == 2:
                    pe.wait_ge(z32_done, 3)
                if t == 6:
                    pe.wait_ge(onehots, 1)
                if t == 7:
                    pe.wait_ge(rows_done, 2)
                rows = slice(t * P, (t + 1) * P)
                product(ps[:, down_bank[t], :],
                        parts(lambda c: z_hi[:, c, rows], lambda c: z_lo[:, c, rows],
                              lambda c: wd_hi[0][:, c, :], lambda c: wd_lo[0][:, c, :]), range(IC)).then_inc(d_ps, 1)

            shared_unit(1)
            pe.wait_ge(sel_done, 1)
            for t in range(NT + 1):
                for k in range(min(t + 1, NT)):
                    last = pe.matmul(ps[:, 6, t * E:(t + 1) * E], below[:, :] if k == t else ones[:, :], sel[:, k, :],
                                     start=(k == 0), stop=(k == min(t, NT - 1)))
            last.then_inc(rank_ps, 1)
            for u in range(2, 4):
                shared_unit(u)
            for t in range(4):
                shared_down(t)
            pe.wait_ge(onehots, 3)
            pe.wait_ge(tokens_set, NT)
            for k in range(NTK):
                last = pe.matmul(ps[0:SW, 7, 0:NS], on_b[:, k, :], on_tok[:, k, :], start=(k == 0), stop=(k == NTK - 1))
            last.then_inc(slot_ps, 1)
            for t in range(4, 7):
                shared_down(t)

            def transpose_slots(r, par, n):
                pe.wait_ge(gathered[par], slots_read(r, par))
                if n >= 2:
                    pe.wait_ge(tT_split, 2 * (r - 1))
                for j in range(2):
                    for k in range(2):
                        for h in range(2):
                            c = 2 * j + k
                            col = k * TS + h * SW
                            last = pe.transpose(ps[:, 4 + j, col:col + SW], h_slot[par][0:SW, h, c * P:(c + 1) * P],
                                                ident[0:SW, 0:SW])
                    last.then_inc(tT_ps, 1)

            def gate_up(r, par, n):
                pe.wait_ge(tT_split, 2 * r)
                pe.wait_ge(wgu_split, KC * r + KC)
                for c in range(IC):
                    if n >= 2:
                        pe.wait_ge(tz32_done, 2 * (r - 2) + c + 1)
                    for gu in range(2):
                        w = slice(gu * I + c * P, gu * I + (c + 1) * P)
                        last = product(ps[:, c, 256 * gu:256 * gu + TS],
                                       parts(lambda k: wgu_hi[par][:, k, w], lambda k: wgu_lo[par][:, k, w],
                                             lambda k: tT_hi[par][:, k, :], lambda k: tT_lo[par][:, k, :]), range(KC))
                    last.then_inc(tgu_ps, 1)
                    if n == 1 and c == 0:
                        transpose_slots(2, 0, 2)

            def down(r, par, n):
                pe.wait_ge(wd_split, IC * r + IC)
                pe.wait_ge(tz_split, 2 * r)
                for h in range(2):
                    if n >= 2:
                        pe.wait_ge(y_done, 2 * (r - 2) + h + 1)
                    rows = slice(h * SW, (h + 1) * SW)
                    product(ps[0:SW, 6 + h, :],
                            parts(lambda c: tz_hi[par][:, c, rows], lambda c: tz_lo[par][:, c, rows],
                                  lambda c: wd_hi[par][:, c, :], lambda c: wd_lo[par][:, c, :]),
                            range(IC)).then_inc(td_ps, 1)

            def step(r, par, n):
                if 1 < n < TILES:
                    transpose_slots(r + 1, 1 - par, n + 1)
                if n == 1:
                    pe.wait_ge(d_added, 4)
                if n == 2:
                    pe.wait_ge(d_added, NT)
                gate_up(r, par, n)
                if n >= 2:
                    down(r - 1, 1 - par, n - 1)

            pe.wait_ge(d_added, 2)
            transpose_slots(1, 1, 1)
            shared_down(7)
            rounds(pe, step)
            down(TILES, TILES % 2, TILES)


def kernel(x, ctx_4096, mask_1x1xSxS2_ff0, L0_xattn_Wq, L0_xattn_Wk, L0_xattn_Wv, L0_xattn_Wo,
           L0_xattn_q_norm_w, L0_xattn_k_norm_w, L0_ffn_gate_w, L0_ffn_bias, L0_ffn_Wg, L0_ffn_Wu,
           L0_ffn_Wd, L0_ffn_Sg, L0_ffn_Su, L0_ffn_Sd):
    import numpy as np
    import concourse.bacc as bacc
    from concourse.bass_utils import run_bass_kernel_spmd

    def chunked(w):
        w = np.swapaxes(w, -1, -2)
        return np.swapaxes(w.reshape(*w.shape[:-2], w.shape[-2] // P, P, w.shape[-1]), -3, -2)

    a = [np.asarray(v) for v in (L0_xattn_Wq, L0_xattn_Wk, L0_xattn_Wv, L0_xattn_Wo, L0_ffn_Wg, L0_ffn_Wu,
                                 L0_ffn_Wd, L0_ffn_Sg, L0_ffn_Su, L0_ffn_Sd)]
    Wq, Wk, Wv, Wo, Wg, Wu, Wd, Sg, Su, Sd = a
    kv = np.concatenate([Wk.reshape(G, HD, D), Wv.reshape(G, HD, D)], axis=1)
    gu = np.concatenate([np.concatenate([Wg, Sg[None]]), np.concatenate([Wu, Su[None]])], axis=1)
    down = np.concatenate([Wd, Sd[None]])
    arrays = {
        "x_half": np.asarray(x).reshape(B, S, 2, HALF).transpose(2, 1, 0, 3).reshape(P, B * HALF),
        "ctx_t": np.asarray(ctx_4096).reshape(T, KC, P).transpose(2, 1, 0).reshape(P, KC * T),
        "mask": np.asarray(mask_1x1xSxS2_ff0).reshape(S, S),
        "wq": chunked(Wq.reshape(G, HG * HD, D)),
        "wkv": chunked(kv),
        "wo": Wo.reshape(D, G, HG, HD).transpose(1, 3, 2, 0),
        "qk_norm": np.stack([np.asarray(L0_xattn_q_norm_w), np.asarray(L0_xattn_k_norm_w)], axis=1),
        "gate_t": chunked(np.asarray(L0_ffn_gate_w)).reshape(P, KC * E),
        "bias": np.broadcast_to(np.asarray(L0_ffn_bias), (P, E)),
        "wgu": chunked(gu),
        "wd": chunked(down),
    }
    nc = bacc.Bacc("TRN2", target_bir_lowering=False, num_devices=1)
    arrays = {f"in_{k}": np.ascontiguousarray(v) for k, v in arrays.items()}
    args = [nc.dram_tensor(k, v.shape, F32, kind="ExternalInput").ap() for k, v in arrays.items()]
    h_rows = nc.dram_tensor("h_rows", (T, HROW), F32).ap()
    out = nc.dram_tensor("out_x", (T + TS, D), F32, kind="ExternalOutput").ap()
    decoder_kernel(nc, *args, h_rows, out)
    r = run_bass_kernel_spmd(nc, [arrays], core_ids=[0])
    return r.results[0]["out_x"][0:T].reshape(B, S, D)
```
